# Optimizing a Trainium2 kernel written in Bass

```python
import numpy as np
import jax
import jax.numpy as jnp

def _softmax(x, axis=-1):
    return jax.nn.softmax(x, axis=axis)

def _gelu(x):
    return jax.nn.gelu(x, approximate=True)

def _silu(x):
    return jax.nn.silu(x)

def _sigmoid(x):
    return jax.nn.sigmoid(x)

def _layernorm(x, axis=-1, eps=1e-05):
    m = jnp.mean(x, axis=axis, keepdims=True)
    v = jnp.var(x, axis=axis, keepdims=True)
    return (x - m) / jnp.sqrt(v + eps)

def _scatter_add(tgt, idx, src, axis=0):
    return tgt.at[idx].add(src)

def _segment_sum(src, seg, n):
    return jax.ops.segment_sum(src, seg, n)
kernel_name = 'mk_perceiver_d1_seqx_r4_73dd31'

def setup_inputs(seed: int=0):
    np.random.seed(seed)
    _w = jnp.asarray

    def _rec_inputs():
        import jax
        import jax.numpy as jnp
        _rk = jax.random.key(seed)
        x = -0.000125 + 0.9999 * jax.random.normal(jax.random.fold_in(_rk, 1), (1, 128, 512), jnp.float32)
        _lenS = 128 - jax.random.randint(jax.random.fold_in(_rk, 7), (1,), 0, max(1, 128 // 4) + 1, jnp.int32)
        _lenS2 = 12544 - jax.random.randint(jax.random.fold_in(_rk, 8), (1,), 0, max(1, 12544 // 4) + 1, jnp.int32)
        _ctx_2048P = jax.random.normal(jax.random.fold_in(_rk, 11), (1, 16, 512), jnp.float32)
        _ctx_2048c = jax.random.dirichlet(jax.random.fold_in(_rk, 511), 0.3 * jnp.ones((16,), jnp.float32), (1, 12544))
        _ctx_2048t = jnp.einsum('bsk,bkd->bsd', _ctx_2048c, _ctx_2048P)
        _ctx_2048t = _ctx_2048t * jax.lax.rsqrt(jnp.mean(jnp.square(_ctx_2048t)) + 1e-12) * 0.953939
        ctx_2048 = -1.52775e-05 + 0.999936 * (_ctx_2048t + 0.3 * jax.random.normal(jax.random.fold_in(_rk, 611), (1, 12544, 512), jnp.float32))
        _validS = jnp.arange(128)[None, :] < _lenS[:, None]
        _validS2 = jnp.arange(12544)[None, :] < _lenS2[:, None]
        _causal = jnp.tril(jnp.ones((128, 128), dtype=bool))
        mask_BxS2_ff1 = jnp.where(jnp.ones((1, 12544), dtype=bool), 1.0, 0.0).astype(jnp.float32)
        return (x, ctx_2048, mask_BxS2_ff1)
    x, ctx_2048, mask_BxS2_ff1 = _rec_inputs()

    def _L0_xattn_setup():
        import jax, jax.numpy as jnp
        import numpy as np
        H = 512
        NH = 16
        HD = H // NH
        FD = 64
        key = jax.random.key(seed)
        ks = jax.random.split(key, 12)
        B, S = (4, 1024)
        s = 1.0 / np.sqrt(H)
        sf = 1.0 / np.sqrt(HD)
        return {'query': jax.random.normal(ks[0], (B, S, H), jnp.float32), 'key': jax.random.normal(ks[1], (B, S, H), jnp.float32), 'value': jax.random.normal(ks[2], (B, S, H), jnp.float32), 'attention_mask': jnp.ones((B, S), jnp.float32), 'Wq': jax.random.normal(ks[3], (H, H), jnp.float32) * s, 'bq': jnp.zeros((H,), jnp.float32), 'Wk': jax.random.normal(ks[4], (H, H), jnp.float32) * s, 'bk': jnp.zeros((H,), jnp.float32), 'Wv': jax.random.normal(ks[5], (H, H), jnp.float32) * s, 'bv': jnp.zeros((H,), jnp.float32), 'Wqf': jax.random.normal(ks[6], (FD, HD), jnp.float32) * sf, 'Wkf': jax.random.normal(ks[7], (FD, HD), jnp.float32) * sf, 'Wo': jax.random.normal(ks[8], (H, H), jnp.float32) * s, 'bo': jnp.zeros((H,), jnp.float32)}
    _L0_xattn_all = _L0_xattn_setup()
    _L0_xattn_in = {k: v for k, v in _L0_xattn_all.items() if k in ('Wq', 'bq', 'Wk', 'bk', 'Wv', 'bv', 'Wqf', 'Wkf', 'Wo', 'bo')}
    del _L0_xattn_all

    def _L0_attn_setup():
        import jax, jax.numpy as jnp
        import numpy as np
        EPS = 1.1920929e-07

        def _rms(x):
            return x * jax.lax.rsqrt(jnp.mean(x * x, axis=-1, keepdims=True) + EPS)
        key = jax.random.key(seed)
        k0, k1, k2, k3 = jax.random.split(key, 4)
        B, S, D, DFF = (4, 512, 512, 2048)
        x = jax.random.normal(k0, (B, S, D), dtype=jnp.float32)
        w_qkv = jax.random.normal(k1, (3 * D, D), dtype=jnp.float32) * 0.02
        w_swiglu = jax.random.normal(k2, (2 * DFF, D), dtype=jnp.float32) * 0.02
        w_out = jax.random.normal(k3, (D, DFF), dtype=jnp.float32) * 0.02
        return {'x': x, 'w_qkv': w_qkv, 'w_swiglu': w_swiglu, 'w_out': w_out}
    _L0_attn_all = _L0_attn_setup()
    _L0_attn_in = {k: v for k, v in _L0_attn_all.items() if k in ('w_qkv', 'w_swiglu', 'w_out')}
    del _L0_attn_all

    def _L0_ffn_setup():
        import jax, jax.numpy as jnp
        import numpy as np
        DIM = 512
        HIDDEN = 2048
        NUM_EXPERTS = 2
        BATCH, SEQ = (4, 256)
        key = jax.random.key(seed)
        k1, k2, k3, k4 = jax.random.split(key, 4)
        x = jax.random.normal(k1, (BATCH, SEQ, DIM), dtype=jnp.float32)
        w_router = jax.random.normal(k2, (NUM_EXPERTS, DIM), dtype=jnp.float32) * (1.0 / np.sqrt(DIM))
        w_fc = jax.random.normal(k3, (NUM_EXPERTS, HIDDEN, DIM), dtype=jnp.float32) * (1.0 / np.sqrt(DIM))
        w_proj = jax.random.normal(k4, (NUM_EXPERTS, DIM, HIDDEN), dtype=jnp.float32) * (1.0 / np.sqrt(HIDDEN))
        return {'x': x, 'w_router': w_router, 'w_fc': w_fc, 'w_proj': w_proj}
    _L0_ffn_all = _L0_ffn_setup()
    _L0_ffn_in = {k: v for k, v in _L0_ffn_all.items() if k in ('w_router', 'w_fc', 'w_proj')}
    del _L0_ffn_all
    return {'x': x, 'ctx_2048': ctx_2048, 'mask_BxS2_ff1': mask_BxS2_ff1, 'L0_xattn_Wq': _L0_xattn_in['Wq'], 'L0_xattn_bq': _L0_xattn_in['bq'], 'L0_xattn_Wk': _L0_xattn_in['Wk'], 'L0_xattn_bk': _L0_xattn_in['bk'], 'L0_xattn_Wv': _L0_xattn_in['Wv'], 'L0_xattn_bv': _L0_xattn_in['bv'], 'L0_xattn_Wqf': _L0_xattn_in['Wqf'], 'L0_xattn_Wkf': _L0_xattn_in['Wkf'], 'L0_xattn_Wo': _L0_xattn_in['Wo'], 'L0_xattn_bo': _L0_xattn_in['bo'], 'L0_attn_w_qkv': _L0_attn_in['w_qkv'], 'L0_attn_w_swiglu': _L0_attn_in['w_swiglu'], 'L0_attn_w_out': _L0_attn_in['w_out'], 'L0_ffn_w_router': _L0_ffn_in['w_router'], 'L0_ffn_w_fc': _L0_ffn_in['w_fc'], 'L0_ffn_w_proj': _L0_ffn_in['w_proj']}

def reference(x, ctx_2048, mask_BxS2_ff1, L0_xattn_Wq, L0_xattn_bq, L0_xattn_Wk, L0_xattn_bk, L0_xattn_Wv, L0_xattn_bv, L0_xattn_Wqf, L0_xattn_Wkf, L0_xattn_Wo, L0_xattn_bo, L0_attn_w_qkv, L0_attn_w_swiglu, L0_attn_w_out, L0_ffn_w_router, L0_ffn_w_fc, L0_ffn_w_proj):
    import jax
    import jax.numpy as jnp

    def _L0_xattn_ref(query, key, value, attention_mask, Wq, bq, Wk, bk, Wv, bv, Wqf, Wkf, Wo, bo):
        import jax, jax.numpy as jnp
        import numpy as np
        H = 512
        NH = 16
        HD = H // NH
        FD = 64
        B, Sq, _ = query.shape
        Sk = key.shape[1]

        def heads(x, W, b, S):
            return (x @ W.T + b).reshape(B, S, NH, HD).transpose(0, 2, 1, 3)
        q = heads(query, Wq, bq, Sq)
        k = heads(key, Wk, bk, Sk)
        v = heads(value, Wv, bv, Sk)
        q_prime = jax.nn.relu(jnp.einsum('bhnd,fd->bhnf', q, Wqf))
        k_prime = jax.nn.relu(jnp.einsum('bhnd,fd->bhnf', k, Wkf))
        k_prime = k_prime * attention_mask[:, None, :, None]
        kv = jnp.einsum('bhnf,bhne->bhfe', k_prime, v)
        qkv = jnp.einsum('bhmf,bhfe->bhme', q_prime, kv)
        k_sum = jnp.sum(k_prime, axis=2)
        qk_sum = jnp.einsum('bhmf,bhf->bhm', q_prime, k_sum)[..., None]
        out = qkv / (qk_sum + 1e-08)
        out = out.transpose(0, 2, 1, 3).reshape(B, Sq, H)
        return out @ Wo.T + bo

    def _L0_attn_ref(x, w_qkv, w_swiglu, w_out):
        import jax, jax.numpy as jnp
        import numpy as np
        EPS = 1.1920929e-07

        def _rms(x):
            return x * jax.lax.rsqrt(jnp.mean(x * x, axis=-1, keepdims=True) + EPS)
        qkv = _rms(x) @ w_qkv.T
        q, k, v = jnp.split(qkv, 3, axis=-1)
        q = _rms(q)
        k = _rms(k)
        w = jnp.exp(k)
        kv_cum = jnp.cumsum(w * v, axis=1)
        w_cum = jnp.cumsum(w, axis=1)
        y = jax.nn.sigmoid(q) * (kv_cum / (w_cum + 1e-06))
        uv = y @ w_swiglu.T
        u, g = jnp.split(uv, 2, axis=-1)
        return x + u * jax.nn.silu(g) @ w_out.T

    def _L0_ffn_ref(x, w_router, w_fc, w_proj):
        import jax, jax.numpy as jnp
        import numpy as np
        DIM = 512
        HIDDEN = 2048
        NUM_EXPERTS = 2
        BATCH, SEQ = (4, 256)
        bsz, seq, dim = x.shape
        num_experts = w_router.shape[0]
        x_flat = x.reshape(-1, dim)
        logits = x_flat @ w_router.T
        probs = jax.nn.softmax(logits, axis=-1)
        top_idx = jnp.argmax(probs, axis=-1)
        top_weight = jnp.take_along_axis(probs, top_idx[:, None], axis=1)[:, 0]
        h = jnp.einsum('nd,ehd->enh', x_flat, w_fc)
        a = jnp.square(jnp.where(h >= 0, h, 0.5 * h))
        expert_out = jnp.einsum('enh,edh->end', a, w_proj)
        mask = (top_idx[None, :] == jnp.arange(num_experts)[:, None]).astype(x.dtype)
        out = jnp.einsum('end,en->nd', expert_out, mask * top_weight[None, :])
        return out.reshape(bsz, seq, dim)
    x = x + _L0_xattn_ref(_layernorm(x, axis=-1), ctx_2048, ctx_2048, mask_BxS2_ff1, L0_xattn_Wq, L0_xattn_bq, L0_xattn_Wk, L0_xattn_bk, L0_xattn_Wv, L0_xattn_bv, L0_xattn_Wqf, L0_xattn_Wkf, L0_xattn_Wo, L0_xattn_bo)
    x = x + _L0_attn_ref(_layernorm(x, axis=-1), L0_attn_w_qkv, L0_attn_w_swiglu, L0_attn_w_out)
    x = x + _L0_ffn_ref(_layernorm(x, axis=-1), L0_ffn_w_router, L0_ffn_w_fc, L0_ffn_w_proj)
    return x

_drawn_inputs = setup_inputs


def setup_inputs(seed=0):
    import zlib

    import numpy as np

    out = dict(_drawn_inputs(seed))
    spreads = {'L0_xattn_bq': (0.0, 0.8),
     'L0_xattn_bk': (0.0, 0.8),
     'L0_xattn_bv': (0.0, 0.1),
     'L0_xattn_bo': (0.0, 0.1)}
    factors = {'L0_attn_w_qkv': 8.0,
     'L0_attn_w_swiglu': 8.0,
     'L0_attn_w_out': 8.0,
     'L0_ffn_w_router': 6.656,
     'L0_ffn_w_fc': 6.157,
     'L0_ffn_w_proj': 5.406}
    for name, (base, spread) in spreads.items():
        noise = np.random.default_rng([zlib.crc32(name.encode()), seed]).standard_normal(out[name].shape)
        drawn = base * np.exp(spread * noise) if base else spread * noise
        out[name] = jnp.asarray(drawn.astype(out[name].dtype))
    for name, factor in factors.items():
        out[name] = (out[name] * factor).astype(out[name].dtype)
    return out
```

```python
import concourse.bass as bass
from concourse import mybir
from contextlib import ExitStack

P = 128
D = 512
KC = D // P
NH = 16
HD = D // NH
FD = 64
NF = NH * FD
S_CTX = 12544
CHUNK = 256
TILES = CHUNK // P
NC = S_CTX // CHUNK
NT = S_CTX // P
GRP = P // HD
NG = NH // GRP
GF = GRP * FD
NPAIR = NF // P
DFF = 2048
LN_EPS = 1e-5
RMS_EPS = 1.1920929e-07
DEN_EPS = 1e-8
CUM_EPS = 1e-6

WO_AT, QKV_AT, SWI_AT = 0, KC * D, KC * D + KC * 3 * D
EARLY = SWI_AT + KC * 2 * DFF
PIECE = 1024
NPIECE = EARLY // PIECE
STAGE = EARLY - 8 * PIECE


def perceiver_kernel(nc, x_in, ctx_in, mask_in, wq_in, bq_in, wk_in, bk_in, wv_in, bv_in, bdq_in, bdk_in,
                     bo_in, early_in, wout_in, wr_in, fc_in, proj_in, ident_in, tri_in, sel_in, out):
    f32, f32r = mybir.dt.float32, mybir.dt.float32r
    ALU, ACT, AX = mybir.AluOpType, mybir.ActivationFunctionType, mybir.AxisListType

    ctx = ExitStack()
    with ctx:
        def sb(name, shape, dt=f32, where=ctx):
            return where.enter_context(nc.sbuf_tensor(name, shape, dt))

        def sem(name):
            return ctx.enter_context(nc.semaphore(name))

        early = sb("early", [P, EARLY])
        x_sb = sb("x_sb", [P, D])
        ident = sb("ident", [P, P])
        mask = sb("mask", [P, NT])
        bias_cols = sb("bias_cols", [P, 2 * KC])
        bdq = sb("bdq", [P, GF])
        qf_T = sb("qf_T", [P, NPAIR, P])
        ksum_acc = sb("ksum_acc", [P, NF])
        kv_blocks = sb("kv_blocks", [P, NG, GF])
        stat = sb("stat", [P, 32])
        half = sb("half", [P, 1])
        ones = sb("ones", [P, 1])
        ksum = sb("ksum", [P, NPAIR])
        ksum_bd = sb("ksum_bd", [P, NPAIR, NH])
        den = sb("den", [P, NH])
        rden = sb("rden", [P, NH])
        logit = sb("logit", [P, 8])
        w_router = sb("w_router", [P, KC, 2])

        phase = ExitStack()
        ctx_raw = sb("ctx_raw", [P, KC, CHUNK], f32, phase)
        ctx_hi = sb("ctx_hi", [P, 2, KC, CHUNK], f32r, phase)
        ctx_lo = sb("ctx_lo", [P, 2, KC, CHUNK], f32r, phase)
        wk_hi = sb("wk_hi", [P, KC, D], f32r, phase)
        wk_lo = sb("wk_lo", [P, KC, D], f32r, phase)
        wv_hi = sb("wv_hi", [P, KC, D], f32r, phase)
        wv_lo = sb("wv_lo", [P, KC, D], f32r, phase)
        bd_hi = sb("bd_hi", [P, GF], f32r, phase)
        bd_lo = sb("bd_lo", [P, GF], f32r, phase)
        k_hi = sb("k_hi", [P, NG, CHUNK], f32r, phase)
        k_lo = sb("k_lo", [P, NG, CHUNK], f32r, phase)
        kf = sb("kf", [P, TILES, NF], f32, phase)
        kf_hi = sb("kf_hi", [P, TILES, NF], f32r, phase)
        kf_lo = sb("kf_lo", [P, TILES, NF], f32r, phase)
        v_hi = sb("v_hi", [P, TILES, D], f32r, phase)
        v_lo = sb("v_lo", [P, TILES, D], f32r, phase)
        phase.close()

        w_out = sb("w_out", [P, DFF // P, D])
        fc0 = sb("fc0", [P, KC, DFF])
        bv = sb("bv", [P, D])
        bo = sb("bo", [P, D])
        tri = sb("tri", [P, P])
        sel = sb("sel", [P, NPAIR, NH])
        kv_T = sb("kv_T", [P, NPAIR, P])
        att = sb("att", [P, D])
        act_T = sb("act_T", [P, KC, P])
        x1 = sb("x1", [P, D])
        z1 = sb("z1", [P, D])
        eq = sb("eq", [P, D])
        gate = sb("gate", [P, 2, D])
        hid = sb("hid", [P, 2, D])
        hid_T = sb("hid_T", [P, KC, P])
        wexp = kv_T[:, 0:4, :].rearrange("p a b -> p (a b)")
        wval = kv_T[:, 4:8, :].rearrange("p a b -> p (a b)")
        hid_T2 = [hid_T, kv_T[:, 0:4, :]]

        w_o = early[:, WO_AT:QKV_AT].rearrange("p (k n) -> p k n", k=KC)
        w_qkv = early[:, QKV_AT:SWI_AT].rearrange("p (k n) -> p k n", k=KC)
        w_swi = early[:, SWI_AT:EARLY].rearrange("p (k n) -> p k n", k=KC)
        late = early[:, SWI_AT:EARLY]
        proj0 = late[:, 0:KC * DFF].rearrange("p (k n) -> p k n", n=D)
        fc1 = late[:, KC * DFF:2 * KC * DFF].rearrange("p (k n) -> p k n", k=KC)

        def staged(at, n):
            return early[:, STAGE + at:STAGE + at + n]
        wq = staged(0, KC * D).rearrange("p (k n) -> p k n", k=KC)
        wk_raw = staged(KC * D, KC * D).rearrange("p (k n) -> p k n", k=KC)
        wv_raw = staged(2 * KC * D, KC * D).rearrange("p (k n) -> p k n", k=KC)
        z0 = staged(3 * KC * D, D)
        z0_T = staged(3 * KC * D + D, D).rearrange("p (k t) -> p k t", k=KC)
        q_T = staged(3 * KC * D + 2 * D, D).rearrange("p (k t) -> p k t", k=KC)
        bdk = staged(3 * KC * D + 3 * D, GF)

        def bank(name):
            return ctx.enter_context(nc.psum_tensor(name, [P, 512], f32))
        k_ps = [bank("k_ps0"), bank("k_ps1")]
        v_ps = [bank("v_ps0"), bank("v_ps1")]
        f_ps = [bank("f_ps0"), bank("f_ps1")]
        kv_ps = [bank("kv_ps0"), bank("kv_ps1")]

        x_loaded = sem("x_loaded")
        ident_loaded = sem("ident_loaded")
        wk_loaded = sem("wk_loaded")
        bdk_loaded = sem("bdk_loaded")
        bias_loaded = sem("bias_loaded")
        wq_loaded = sem("wq_loaded")
        wv_loaded = sem("wv_loaded")
        mask_loaded = sem("mask_loaded")
        ctx_loaded = sem("ctx_loaded")
        early_loaded = sem("early_loaded")
        tail_small_loaded = sem("tail_small_loaded")
        wout_loaded = sem("wout_loaded")
        fc0_loaded = sem("fc0_loaded")
        proj0_loaded = sem("proj0_loaded")
        fc1_loaded = sem("fc1_loaded")
        proj1_loaded = sem("proj1_loaded")
        out_stored = sem("out_stored")
        consts_set = sem("consts_set")
        chain = sem("vector_chain")
        act_chain = sem("scalar_chain")
        var_ready = sem("var_ready")
        rstd_ready = sem("rstd_ready")
        wk_hi_ready = sem("wk_hi_ready")
        wk_lo_ready = sem("wk_lo_ready")
        bd_hi_ready = sem("bd_hi_ready")
        bd_lo_ready = sem("bd_lo_ready")
        wv_hi_ready = sem("wv_hi_ready")
        wv_lo_ready = sem("wv_lo_ready")
        z0_ready = sem("z0_ready")
        z0T_done = sem("z0T_done")
        z0T_ready = sem("z0T_ready")
        q_done = sem("q_done")
        q_ready = sem("q_ready")
        qf_done = sem("qf_done")
        qf_ready = sem("qf_ready")
        ctx_hi_ready = sem("ctx_hi_ready")
        ctx_lo_ready = sem("ctx_lo_ready")
        k_done = sem("k_done")
        k_hi_ready = sem("k_hi_ready")
        k_lo_ready = sem("k_lo_ready")
        v_done = sem("v_done")
        v_hi_ready = sem("v_hi_ready")
        v_lo_ready = sem("v_lo_ready")
        f_done = sem("f_done")
        kf_ready = sem("kf_ready")
        kf_hi_ready = sem("kf_hi_ready")
        kf_lo_ready = sem("kf_lo_ready")
        ksum_added = sem("ksum_added")
        kv_done = sem("kv_done")
        ksumT_done = sem("ksumT_done")
        kvb_ready = sem("kvb_ready")
        kvT_done = sem("kvT_done")
        kvT_ready = sem("kvT_ready")
        ksum_bd_ready = sem("ksum_bd_ready")
        den_done = sem("den_done")
        num_done = sem("num_done")
        act_ready = sem("act_ready")
        actT_done = sem("actT_done")
        actT_ready = sem("actT_ready")
        o_done = sem("o_done")
        qkv_done = sem("qkv_done")
        rq_ready = sem("rq_ready")
        squares_ready = sem("squares_ready")
        expq_ready = sem("expq_ready")
        expk_ready = sem("expk_ready")
        wval_ready = sem("wval_ready")
        cum_done = sem("cum_done")
        g_done = sem("g_done")
        u_done = sem("u_done")
        expg_ready = sem("expg_ready")
        hid_ready = sem("hid_ready")
        hidT_done = sem("hidT_done")
        hidT_ready = sem("hidT_ready")
        down_done = sem("down_done")
        logit_done = sem("logit_done")
        logit_neg_ready = sem("logit_neg_ready")
        expl_ready = sem("expl_ready")
        fc_done = sem("fc_done")
        fc_half_ready = sem("fc_half_ready")
        out_ready = sem("out_ready")

        block = ctx.enter_context(nc.Block())


        @block.sync
        def _(sp):
            sp.dma_start(x_sb[:, :], x_in).then_inc(x_loaded, 16)
            sp.dma_start(wk_raw, wk_in).then_inc(wk_loaded, 16)
            sp.dma_start(ident[:, :], ident_in).then_inc(ident_loaded, 16)
            sp.dma_start(ctx_raw[:, :, :], ctx_in[0, :, :, :]).then_inc(ctx_loaded, 16)

            def load_chunk(c):
                sp.wait_ge(ctx_lo_ready, c)
                sp.dma_start(ctx_raw[:, :, :], ctx_in[c, :, :, :]).then_inc(ctx_loaded, 16)

            load_chunk(1)
            sp.wait_ge(wv_lo_ready, 1)
            sp.wait_ge(bd_lo_ready, 1)
            sp.wait_ge(qf_done, 2)
            with sp.Fori(2, 2 + NPIECE) as c:
                load_chunk(c)
                sp.dma_start(early[:, bass.ds((c - 2) * PIECE, PIECE)], early_in[c - 2, :, :])\
                  .then_inc(early_loaded, 16)
            with sp.Fori(2 + NPIECE, NC) as c:
                load_chunk(c)
            sp.wait_ge(kv_done, NC)
            sp.wait_ge(ksum_added, NT)
            sp.dma_start(bv[:, :], bv_in).then_inc(tail_small_loaded, 16)
            sp.dma_start(bo[:, :], bo_in).then_inc(tail_small_loaded, 16)
            sp.dma_start(tri[:, :], tri_in).then_inc(tail_small_loaded, 16)
            sp.dma_start(sel[:, :, :], sel_in).then_inc(tail_small_loaded, 16)
            sp.dma_start(w_router[:, :, :], wr_in).then_inc(tail_small_loaded, 16)
            sp.dma_start(w_out[:, :, :], wout_in).then_inc(wout_loaded, 16)
            sp.dma_start(fc0[:, :, :], fc_in[0, :, :, :]).then_inc(fc0_loaded, 16)
            sp.wait_ge(u_done, 4)
            sp.dma_start(proj0, proj_in[0, :, :, :]).then_inc(proj0_loaded, 16)
            sp.dma_start(fc1, fc_in[1, :, :, :]).then_inc(fc1_loaded, 16)
            sp.wait_ge(down_done, 1)
            sp.dma_start(w_out[:, :, :], proj_in[1, :, :, :]).then_inc(proj1_loaded, 16)
            sp.wait_ge(out_ready, 1)
            sp.dma_start(out[0, :, :], hid[:, 0, :]).then_inc(out_stored, 16)
            sp.wait_ge(out_stored, 16)

        @block.gpsimd
        def _(pool):
            pool.memset(half[:, :], -0.5).then_inc(consts_set, 1)
            pool.memset(ones[:, :], 1.0).then_inc(consts_set, 1)
            pool.memset(ksum_acc[:, :], 0.0).then_inc(consts_set, 1)
            pool.memset(kv_blocks[:, :, :], 0.0).then_inc(consts_set, 1)

            def rstd(n, col, m):
                pool.wait_ge(var_ready, n)
                pool.tensor_tensor(stat[:, col:col + m], stat[:, col:col + m],
                                   half[:, 0:1].to_broadcast([P, m]), ALU.pow).then_inc(rstd_ready, 1)

            def split_ctx_low(c, s):
                pool.wait_ge(ctx_hi_ready, c + 1)
                pool.tensor_tensor(ctx_lo[:, s, :, :], ctx_raw[:, :, :], ctx_hi[:, s, :, :].bitcast(f32),
                                   ALU.subtract).then_inc(ctx_lo_ready, 1)

            def add_features(n, t, first=False):
                pool.wait_ge(kf_ready, 2 * n + 2)
                pool.wait_ge(consts_set, 4) if first else pool.wait_ge(ksum_added, n)
                pool.tensor_tensor(ksum_acc[:, :], ksum_acc[:, :], kf[:, t, :], ALU.add).then_inc(ksum_added, 1)

            def period(c, s, first=False, last=False):
                if not last:
                    split_ctx_low(c + 1, 1 - s)
                for t in range(TILES):
                    add_features(TILES * c + t, t, first and t == 0)

            pool.wait_ge(consts_set, 4)
            rstd(1, 8, 1)
            split_ctx_low(0, 0)
            period(0, 0, first=True)
            with pool.Fori(1, NC - 2, 2) as c:
                period(c, 1)
                period(c + 1, 0)
            period(NC - 2, 1)
            period(NC - 1, 0, last=True)
            rstd(2, 8, 1)
            rstd(3, 9, 1)
            rstd(4, 10, 2)
            rstd(5, 8, 1)

        @block.scalar
        def _(act):
            act.dma_start(bdk, bdk_in).then_inc(bdk_loaded, 16)
            act.dma_start(bias_cols[:, 0:KC], bq_in).then_inc(bias_loaded, 16)
            act.dma_start(bias_cols[:, KC:2 * KC], bk_in).then_inc(bias_loaded, 16)
            act.dma_start(wq, wq_in).then_inc(wq_loaded, 16)
            act.dma_start(bdq[:, :], bdq_in).then_inc(wq_loaded, 16)
            act.dma_start(wv_raw, wv_in).then_inc(wv_loaded, 16)
            act.dma_start(mask[:, :], mask_in).then_inc(mask_loaded, 16)

            def split_ctx_high(c, s):
                act.wait_ge(ctx_loaded, 16 * c + 16)
                act.activation(ctx_hi[:, s, :, :], ctx_raw[:, :, :], ACT.Copy).then_inc(ctx_hi_ready, 1)

            def keys_high(c):
                for b in range(2):
                    act.wait_ge(k_done, 2 * c + b + 1)
                    for g in (2 * b, 2 * b + 1):
                        last = act.activation(k_hi[:, g, :], k_ps[b][:, (g % 2) * CHUNK:(g % 2 + 1) * CHUNK],
                                              ACT.Identity, bias=bias_cols[:, KC + g:KC + g + 1])
                    last.then_inc(k_hi_ready, 1)

            def values_high(c, t, first):
                act.wait_ge(v_done, TILES * c + t + 1)
                if not first:
                    act.wait_ge(kv_done, c)
                act.activation(v_hi[:, t, :], v_ps[t][:, :], ACT.Copy).then_inc(v_hi_ready, 1)

            def features_high(c, t):
                act.wait_ge(kf_ready, 2 * (TILES * c + t) + 2)
                act.activation(kf_hi[:, t, :], kf[:, t, :], ACT.Copy).then_inc(kf_hi_ready, 1)

            def period(c, s, first=False, last=False):
                if not last:
                    if not first:
                        act.wait_ge(v_done, TILES * c)
                    split_ctx_high(c + 1, 1 - s)
                for t in range(TILES):
                    values_high(c, t, first)
                    features_high(c, t)
                if not last:
                    keys_high(c + 1)

            act.wait_ge(wk_loaded, 16)
            act.activation(wk_hi[:, :, :], wk_raw, ACT.Copy).then_inc(wk_hi_ready, 1)
            split_ctx_high(0, 0)
            act.wait_ge(bdk_loaded, 16)
            act.activation(bd_hi[:, :], bdk, ACT.Copy).then_inc(bd_hi_ready, 1)
            act.wait_ge(wv_loaded, 16)
            act.activation(wv_hi[:, :, :], wv_raw, ACT.Copy).then_inc(wv_hi_ready, 1)
            act.wait_ge(bias_loaded, 32)
            keys_high(0)
            period(0, 0, first=True)
            with act.Fori(1, NC - 2, 2) as c:
                period(c, 1)
                period(c + 1, 0)
            period(NC - 2, 1)
            period(NC - 1, 0, last=True)

            act.wait_ge(kv_done, NC)
            for h in range(GRP):
                last = act.activation(kv_blocks[HD * h:HD * (h + 1), 2:4, FD * h:FD * (h + 1)],
                                      kv_ps[1][HD * h:HD * (h + 1), :].rearrange("p (g f) -> p g f", g=2)
                                      [:, :, FD * h:FD * (h + 1)], ACT.Copy)
            last.then_inc(kvb_ready, 1)
            act.wait_ge(kvT_done, 1)
            act.wait_ge(ksum_added, NT)
            act.activation(kv_T[:, 0:4, :], f_ps[0][:, :], ACT.Copy).then_inc(kvT_ready, 1)
            act.wait_ge(qkv_done, 1)
            act.activation(eq[:, :], k_ps[0][:, :], ACT.Square, accum_out=stat[:, 10:11]).then_inc(act_chain, 1)
            act.wait_ge(act_chain, 1)
            act.wait_ge(qkv_done, 2)
            act.activation(eq[:, :], k_ps[1][:, :], ACT.Square, accum_out=stat[:, 11:12]).then_inc(squares_ready, 1)
            act.wait_ge(rq_ready, 1)
            act.wait_ge(squares_ready, 1)
            act.activation(eq[:, :], k_ps[0][:, :], ACT.Exp, scale=stat[:, 12:13]).then_inc(expq_ready, 1)
            act.activation(wexp, k_ps[1][:, :], ACT.Exp, scale=stat[:, 11:12]).then_inc(expk_ready, 1)
            for n in range(DFF // D):
                act.wait_ge(g_done, n + 1)
                if n >= 2:
                    act.wait_ge(hid_ready, n - 1)
                act.activation(gate[:, n % 2, :], k_ps[n % 2][:, :], ACT.Exp, scale=-1.0)\
                   .then_inc(expg_ready, 1)
            act.wait_ge(logit_neg_ready, 1)
            act.activation(logit[:, 3:5], logit[:, 0:2], ACT.Exp, bias=logit[:, 2:3]).then_inc(expl_ready, 1)
            for n in range(2 * DFF // D):
                act.wait_ge(fc_done, n + 1)
                if n >= 2:
                    act.wait_ge(hid_ready, DFF // D + n - 1)
                act.activation(gate[:, n % 2, :], k_ps[n % 2][:, :], ACT.Copy, scale=0.5)\
                   .then_inc(fc_half_ready, 1)

        @block.tensor
        def _(pe):
            def three(out_ps, st_hi, st_lo, mv_hi, mv_lo, start, stop, **kw):
                pe.matmul(out_ps, st_lo, mv_hi, start=start, stop=False, **kw)
                pe.matmul(out_ps, st_hi, mv_lo, start=False, stop=False, **kw)
                return pe.matmul(out_ps, st_hi, mv_hi, start=False, stop=stop, **kw)

            def keys(c, s, first=False):
                pe.wait_ge(ctx_lo_ready, c + 1)
                for m in range(NG):
                    if m % 2 == 0 and not first:
                        pe.wait_ge(k_lo_ready, 2 * (c - 1) + m // 2 + 1)
                    for k in range(KC):
                        last = three(k_ps[m // 2][:, (m % 2) * CHUNK:(m % 2 + 1) * CHUNK],
                                     wk_hi[:, k, m * P:(m + 1) * P], wk_lo[:, k, m * P:(m + 1) * P],
                                     ctx_hi[:, s, k, :], ctx_lo[:, s, k, :], k == 0, k == KC - 1)
                    if m % 2 == 1:
                        last.then_inc(k_done, 1)

            def values(c, s, t, first):
                if not first:
                    pe.wait_ge(v_lo_ready, TILES * (c - 1) + t + 1)
                for k in range(KC):
                    last = three(v_ps[t][:, :], ctx_hi[:, s, k, t * P:(t + 1) * P],
                                 ctx_lo[:, s, k, t * P:(t + 1) * P],
                                 wv_hi[:, k, :], wv_lo[:, k, :], k == 0, k == KC - 1)
                last.then_inc(v_done, 1)

            def features(c, t, first):
                n = TILES * c + t
                for g in range(NG):
                    b = g // 2
                    if g % 2 == 0:
                        if t == 0:
                            pe.wait_ge(k_lo_ready, 2 * c + b + 1)
                        if not (first and t == 0):
                            pe.wait_ge(kf_ready, 2 * n + b - 1)
                    out_ps = f_ps[b][:, (g % 2) * GF:(g % 2 + 1) * GF]
                    last = three(out_ps, k_hi[:, g, t * P:(t + 1) * P], k_lo[:, g, t * P:(t + 1) * P],
                                 bd_hi[:, :], bd_lo[:, :], True, True)
                    if g % 2 == 1:
                        last.then_inc(f_done, 1)

            def key_values(c, first, last_chunk):
                for t in range(TILES):
                    pe.wait_ge(v_lo_ready, TILES * c + t + 1)
                    pe.wait_ge(kf_lo_ready, TILES * c + t + 1)
                    for g in range(NG):
                        last = three(kv_ps[g // 2][:, (g % 2) * GF:(g % 2 + 1) * GF],
                                     v_hi[:, t, g * P:(g + 1) * P], v_lo[:, t, g * P:(g + 1) * P],
                                     kf_hi[:, t, g * GF:(g + 1) * GF], kf_lo[:, t, g * GF:(g + 1) * GF],
                                     first and t == 0 and g % 2 == 0,
                                     last_chunk and t == TILES - 1, skip_group_check=True)
                last.then_inc(kv_done, 1)

            def period(c, s, first=False, last=False):
                for t in range(TILES):
                    values(c, s, t, first)
                    if first and t == 0:
                        pe.wait_ge(qf_ready, 2)
                        pe.wait_ge(bd_lo_ready, 1)
                    features(c, t, first)
                if not last:
                    keys(c + 1, 1 - s)
                key_values(c, first, last)

            def transposes(ps, src):
                for k in range(KC):
                    last = pe.transpose(ps[:, k * P:(k + 1) * P], src[:, k * P:(k + 1) * P], ident[:, :])
                return last

            def rows(ps, act_t, w, at, start=True, stop=True):
                for k in range(KC):
                    last = pe.matmul(ps, act_t[:, k, :], w[:, k, at:at + D], start=start and k == 0,
                                     stop=stop and k == KC - 1)
                return last

            pe.wait_ge(ident_loaded, 16)
            pe.wait_ge(z0_ready, 1)
            transposes(kv_ps[0], z0).then_inc(z0T_done, 1)
            pe.wait_ge(wk_lo_ready, 1)
            keys(0, 0, first=True)
            pe.wait_ge(z0T_ready, 1)
            pe.wait_ge(wq_loaded, 32)
            for m in range(KC):
                for k in range(KC):
                    last = pe.matmul(kv_ps[1][:, m * P:(m + 1) * P], wq[:, k, m * P:(m + 1) * P],
                                     z0_T[:, k, :], start=k == 0, stop=k == KC - 1)
            last.then_inc(q_done, 1)
            pe.wait_ge(q_ready, 1)
            for j in range(NPAIR):
                last = pe.matmul(f_ps[j // 4][:, (j % 4) * P:(j % 4 + 1) * P], bdq[:, (j % 2) * P:(j % 2 + 1) * P],
                                 q_T[:, j // 2, :], start=True, stop=True)
                if j % 4 == 3:
                    last.then_inc(qf_done, 1)
            pe.wait_ge(wv_lo_ready, 1)
            period(0, 0, first=True)
            with pe.Fori(1, NC - 2, 2) as c:
                period(c, 1)
                period(c + 1, 0)
            period(NC - 2, 1)
            period(NC - 1, 0, last=True)

            pe.wait_ge(ksum_added, NT)
            for j in range(NPAIR):
                last = pe.matmul(v_ps[0][:, j:j + 1], ksum_acc[:, j * P:(j + 1) * P], ones[:, :],
                                 start=True, stop=True)
            last.then_inc(ksumT_done, 1)
            pe.wait_ge(kvb_ready, 2)
            for j in range(NPAIR):
                last = pe.transpose(f_ps[j // 4][:, (j % 4) * P:(j % 4 + 1) * P],
                                    kv_blocks[:, j // 2, (j % 2) * P:(j % 2 + 1) * P], ident[:, :])
                if j % 4 == 3:
                    last.then_inc(kvT_done, 1)
            pe.wait_ge(ksum_bd_ready, 1)
            for j in range(NPAIR):
                last = pe.matmul(v_ps[1][:, 0:NH], qf_T[:, j, :], ksum_bd[:, j, :], start=j == 0,
                                 stop=j == NPAIR - 1)
            last.then_inc(den_done, 1)
            pe.wait_ge(kvT_ready, 2)
            for j in range(NPAIR):
                last = pe.matmul(k_ps[0][:, (j // 2) * P:(j // 2 + 1) * P], qf_T[:, j, :], kv_T[:, j, :],
                                 start=j % 2 == 0, stop=j % 2 == 1)
            last.then_inc(num_done, 1)

            def turn(n, src, ps):
                pe.wait_ge(act_ready, n)
                transposes(ps, src).then_inc(actT_done, 1)
                pe.wait_ge(actT_ready, n)

            turn(1, att, v_ps[1])
            pe.wait_ge(early_loaded, 16 * NPIECE)
            rows(k_ps[1][:, :], act_T, w_o, 0).then_inc(o_done, 1)

            turn(2, att, v_ps[1])
            for n, ps in enumerate((k_ps[0], k_ps[1], v_ps[0])):
                rows(ps[:, :], act_T, w_qkv, n * D).then_inc(qkv_done, 1)
            pe.wait_ge(tail_small_loaded, 16 * 5)
            pe.wait_ge(expk_ready, 1)
            pe.matmul(f_ps[0][:, :], tri[:, :], wexp, start=True, stop=True).then_inc(cum_done, 1)
            pe.wait_ge(wval_ready, 1)
            pe.matmul(f_ps[1][:, :], tri[:, :], wval, start=True, stop=True).then_inc(cum_done, 1)
            turn(3, att, v_ps[1])

            def hidden_turn(n):
                pe.wait_ge(hid_ready, n + 1)
                if n >= 2:
                    pe.wait_ge(hidT_ready, n - 1)
                transposes(f_ps[n % 2], hid[:, n % 2, :]).then_inc(hidT_done, 1)

            def hidden_down(n, w, at, first, last_one):
                pe.wait_ge(hidT_ready, n + 1)
                for k in range(KC):
                    last = pe.matmul(kv_ps[0][:, :], hid_T2[n % 2][:, k, :], w[:, at + k, :],
                                     start=first and k == 0, stop=last_one and k == KC - 1)
                return last

            nd = DFF // D
            for n in range(nd + 1):
                if n < nd:
                    if n >= 2:
                        pe.wait_ge(hid_ready, n - 1)
                    rows(k_ps[n % 2][:, :], act_T, w_swi, DFF + n * D).then_inc(g_done, 1)
                    if n == 1:
                        pe.wait_ge(hid_ready, 1)
                    rows(v_ps[n % 2][:, :], act_T, w_swi, n * D).then_inc(u_done, 1)
                if n >= 1:
                    hidden_turn(n - 1)
                    if n == 1:
                        pe.wait_ge(wout_loaded, 16)
                    last = hidden_down(n - 1, w_out, (n - 1) * KC, n == 1, n == nd)
            last.then_inc(down_done, 1)

            turn(4, att, v_ps[1])
            for k in range(KC):
                last = pe.matmul(v_ps[0][:, 0:2], act_T[:, k, :], w_router[:, k, :], start=k == 0,
                                 stop=k == KC - 1)
            last.then_inc(logit_done, 1)
            pe.wait_ge(fc0_loaded, 16)
            for n in range(2 * nd + 1):
                if n < 2 * nd:
                    if n == nd:
                        pe.wait_ge(fc1_loaded, 16)
                    if n >= 2:
                        pe.wait_ge(hid_ready, nd + n - 1)
                    rows(k_ps[n % 2][:, :], act_T, fc0 if n < nd else fc1, (n % nd) * D).then_inc(fc_done, 1)
                if n >= 1:
                    m = n - 1
                    hidden_turn(nd + m)
                    if m == 0:
                        pe.wait_ge(proj0_loaded, 16)
                    if m == nd:
                        pe.wait_ge(proj1_loaded, 16)
                    last = hidden_down(nd + m, proj0 if m < nd else w_out, (m % nd) * KC, m == 0, n == 2 * nd)
            last.then_inc(down_done, 1)

        @block.vector
        def _(dve):
            links = [0]

            def link(ins):
                links[0] += 1
                ins.then_inc(chain, 1)
                dve.wait_ge(chain, links[0])

            def layer_norm(n, dst, src):
                link(dve.bn_stats(stat[:, 0:6], src))
                link(dve.bn_aggr(stat[:, 6:8], stat[:, 0:6]))
                dve.tensor_scalar(stat[:, 8:9], stat[:, 7:8], LN_EPS, None, ALU.add).then_inc(var_ready, 1)
                dve.wait_ge(rstd_ready, n)
                return dve.tensor_scalar(dst, src, stat[:, 6:7], stat[:, 8:9], ALU.subtract, ALU.mult)

            def keys_low(c):
                for b in range(2):
                    dve.wait_ge(k_hi_ready, 2 * c + b + 1)
                    for g in (2 * b, 2 * b + 1):
                        last = dve.scalar_tensor_tensor(
                            out=k_lo[:, g, :], in0=k_ps[b][:, (g % 2) * CHUNK:(g % 2 + 1) * CHUNK],
                            scalar=bias_cols[:, KC + g:KC + g + 1], in1=k_hi[:, g, :].bitcast(f32),
                            op0=ALU.add, op1=ALU.subtract)
                    last.then_inc(k_lo_ready, 1)

            def values_low(c, t):
                dve.wait_ge(v_hi_ready, TILES * c + t + 1)
                dve.tensor_tensor(v_lo[:, t, :], v_ps[t][:, :], v_hi[:, t, :].bitcast(f32), ALU.subtract)\
                   .then_inc(v_lo_ready, 1)

            def masked_features(c, t, first):
                n = TILES * c + t
                for b in range(2):
                    dve.wait_ge(f_done, 2 * n + b + 1)
                    if b == 0 and not first:
                        dve.wait_ge(ksum_added, n - 1)
                    dve.tensor_scalar(kf[:, t, b * D:(b + 1) * D], f_ps[b][:, :], 0.0,
                                      mask[:, bass.ds(n, 1)], ALU.max, ALU.mult).then_inc(kf_ready, 1)

            def features_low(c, t):
                dve.wait_ge(kf_hi_ready, TILES * c + t + 1)
                dve.tensor_tensor(kf_lo[:, t, :], kf[:, t, :], kf_hi[:, t, :].bitcast(f32), ALU.subtract)\
                   .then_inc(kf_lo_ready, 1)

            def period(c, first=False, last=False):
                for t in range(TILES):
                    values_low(c, t)
                    masked_features(c, t, first)
                    features_low(c, t)
                if not last:
                    keys_low(c + 1)

            dve.wait_ge(x_loaded, 16)
            layer_norm(1, z0, x_sb[:, :]).then_inc(z0_ready, 1)
            dve.wait_ge(wk_hi_ready, 1)
            dve.tensor_tensor(wk_lo[:, :, :], wk_raw, wk_hi[:, :, :].bitcast(f32), ALU.subtract)\
               .then_inc(wk_lo_ready, 1)
            dve.wait_ge(z0T_done, 1)
            dve.tensor_copy(z0_T, kv_ps[0][:, :].rearrange("p (k t) -> p k t", k=KC)).then_inc(z0T_ready, 1)
            dve.wait_ge(bd_hi_ready, 1)
            dve.tensor_tensor(bd_lo[:, :], bdk, bd_hi[:, :].bitcast(f32), ALU.subtract)\
               .then_inc(bd_lo_ready, 1)
            dve.wait_ge(wv_hi_ready, 1)
            dve.tensor_tensor(wv_lo[:, :, :], wv_raw, wv_hi[:, :, :].bitcast(f32), ALU.subtract)\
               .then_inc(wv_lo_ready, 1)
            dve.wait_ge(bias_loaded, 32)
            keys_low(0)
            dve.wait_ge(q_done, 1)
            for m in range(KC):
                last = dve.tensor_scalar(q_T[:, m, :], kv_ps[1][:, m * P:(m + 1) * P], bias_cols[:, m:m + 1],
                                         None, ALU.add)
            last.then_inc(q_ready, 1)
            for b in range(2):
                dve.wait_ge(qf_done, b + 1)
                dve.tensor_scalar(qf_T[:, 4 * b:4 * b + 4, :], f_ps[b][:, :].rearrange("p (k t) -> p k t", k=4),
                                  0.0, None, ALU.max).then_inc(qf_ready, 1)
            dve.wait_ge(mask_loaded, 16)
            period(0, first=True)
            with dve.Fori(1, NC - 2, 2) as c:
                period(c)
                period(c + 1)
            period(NC - 2)
            period(NC - 1, last=True)

            dve.wait_ge(kv_done, NC)
            for h in range(GRP):
                last = dve.tensor_copy(kv_blocks[HD * h:HD * (h + 1), 0:2, FD * h:FD * (h + 1)],
                                       kv_ps[0][HD * h:HD * (h + 1), :].rearrange("p (g f) -> p g f", g=2)
                                       [:, :, FD * h:FD * (h + 1)])
            last.then_inc(kvb_ready, 1)
            dve.wait_ge(ksumT_done, 1)
            link(dve.tensor_copy(ksum[:, :], v_ps[0][:, 0:NPAIR]))
            dve.wait_ge(tail_small_loaded, 16 * 5)
            for j in range(NPAIR):
                last = dve.tensor_scalar(ksum_bd[:, j, :], sel[:, j, :], ksum[:, j:j + 1], None, ALU.mult)
            last.then_inc(ksum_bd_ready, 1)
            dve.wait_ge(kvT_done, 2)
            dve.tensor_copy(kv_T[:, 4:8, :], f_ps[1][:, :].rearrange("p (k t) -> p k t", k=4))\
               .then_inc(kvT_ready, 1)
            dve.wait_ge(den_done, 1)
            link(dve.tensor_copy(den[:, :], v_ps[1][:, 0:NH]))
            link(dve.tensor_scalar(rden[:, :], den[:, :], DEN_EPS, None, ALU.add))
            link(dve.reciprocal(rden[:, :], rden[:, :]))

            def by_head(a):
                return a.rearrange("p (h e) -> p h e", h=NH)

            def per_head(a):
                return a.unsqueeze(2).to_broadcast([P, NH, HD])
            link(dve.tensor_tensor(by_head(att[:, :]), by_head(bv[:, :]), per_head(den[:, :]), ALU.mult))
            dve.wait_ge(num_done, 1)
            link(dve.tensor_tensor(att[:, :], k_ps[0][:, :], att[:, :], ALU.add))
            dve.tensor_tensor(by_head(att[:, :]), by_head(att[:, :]), per_head(rden[:, :]), ALU.mult)\
               .then_inc(act_ready, 1)

            def turned(n):
                dve.wait_ge(actT_done, n)
                dve.tensor_copy(act_T[:, :, :], v_ps[1][:, :].rearrange("p (k t) -> p k t", k=KC))\
                   .then_inc(actT_ready, 1)
            turned(1)
            link(dve.tensor_tensor(x1[:, :], x_sb[:, :], bo[:, :], ALU.add))
            dve.wait_ge(o_done, 1)
            link(dve.tensor_tensor(x1[:, :], x1[:, :], k_ps[1][:, :], ALU.add))

            link(layer_norm(2, z1[:, :], x1[:, :]))
            link(dve.tensor_tensor(att[:, :], z1[:, :], z1[:, :], ALU.mult))
            link(dve.tensor_reduce(stat[:, 13:14], att[:, :], AX.X, ALU.add))
            dve.tensor_scalar(stat[:, 9:10], stat[:, 13:14], 1.0 / D, RMS_EPS, ALU.mult, ALU.add)\
               .then_inc(var_ready, 1)
            dve.wait_ge(rstd_ready, 3)
            dve.tensor_scalar(att[:, :], z1[:, :], stat[:, 9:10], None, ALU.mult).then_inc(act_ready, 1)
            turned(2)
            dve.wait_ge(squares_ready, 1)
            dve.tensor_scalar(stat[:, 10:12], stat[:, 10:12], 1.0 / D, RMS_EPS, ALU.mult, ALU.add)\
               .then_inc(var_ready, 1)
            dve.wait_ge(rstd_ready, 4)
            dve.tensor_scalar(stat[:, 12:13], stat[:, 10:11], -1.0, None, ALU.mult).then_inc(rq_ready, 1)
            dve.wait_ge(expk_ready, 1)
            dve.wait_ge(qkv_done, 3)
            dve.tensor_tensor(wval, v_ps[0][:, :], wexp, ALU.mult).then_inc(wval_ready, 1)
            dve.wait_ge(expq_ready, 1)
            link(dve.tensor_scalar(eq[:, :], eq[:, :], 1.0, None, ALU.add))
            dve.wait_ge(cum_done, 1)
            link(dve.scalar_tensor_tensor(out=eq[:, :], in0=f_ps[0][:, :], scalar=CUM_EPS, in1=eq[:, :],
                                          op0=ALU.add, op1=ALU.mult))
            link(dve.reciprocal(eq[:, :], eq[:, :]))
            dve.wait_ge(cum_done, 2)
            dve.tensor_tensor(att[:, :], f_ps[1][:, :], eq[:, :], ALU.mult).then_inc(act_ready, 1)
            turned(3)

            def hidden_turned(n):
                dve.wait_ge(hidT_done, n + 1)
                dve.tensor_copy(hid_T2[n % 2][:, :, :], f_ps[n % 2][:, :].rearrange("p (k t) -> p k t", k=KC))\
                   .then_inc(hidT_ready, 1)

            nd = DFF // D
            for n in range(nd):
                dve.wait_ge(expg_ready, n + 1)
                e = gate[:, n % 2, :]
                link(dve.tensor_scalar(e, e, 1.0, None, ALU.add))
                link(dve.reciprocal(e, e))
                link(dve.tensor_tensor(e, k_ps[n % 2][:, :], e, ALU.mult))
                dve.wait_ge(u_done, n + 1)
                dve.tensor_tensor(hid[:, n % 2, :], v_ps[n % 2][:, :], e, ALU.mult).then_inc(hid_ready, 1)
                if n == 0:
                    link(dve.tensor_tensor(x1[:, :], x1[:, :], z1[:, :], ALU.add))
                hidden_turned(n)
            dve.wait_ge(down_done, 1)
            link(dve.tensor_tensor(x1[:, :], x1[:, :], kv_ps[0][:, :], ALU.add))

            layer_norm(5, att[:, :], x1[:, :]).then_inc(act_ready, 1)
            turned(4)
            dve.wait_ge(logit_done, 1)
            link(dve.tensor_copy(logit[:, 0:2], v_ps[0][:, 0:2]))
            link(dve.tensor_reduce(logit[:, 2:3], logit[:, 0:2], AX.X, ALU.max))
            dve.tensor_scalar(logit[:, 2:3], logit[:, 2:3], -1.0, None, ALU.mult).then_inc(logit_neg_ready, 1)
            dve.wait_ge(expl_ready, 1)
            link(dve.tensor_reduce(logit[:, 5:6], logit[:, 3:5], AX.X, ALU.add))
            link(dve.reciprocal(logit[:, 5:6], logit[:, 5:6]))
            link(dve.tensor_scalar(logit[:, 3:5], logit[:, 3:5], logit[:, 5:6], None, ALU.mult))
            link(dve.tensor_tensor(logit[:, 6:7], logit[:, 3:4], logit[:, 4:5], ALU.is_ge))
            link(dve.tensor_scalar(logit[:, 7:8], logit[:, 6:7], -1.0, 1.0, ALU.mult, ALU.add))
            link(dve.tensor_tensor(logit[:, 6:8], logit[:, 6:8], logit[:, 3:5], ALU.mult))

            for n in range(2 * nd):
                e = n // nd
                dve.wait_ge(fc_half_ready, n + 1)
                h = gate[:, n % 2, :]
                link(dve.tensor_tensor(h, k_ps[n % 2][:, :], h, ALU.max))
                dve.scalar_tensor_tensor(out=hid[:, n % 2, :], in0=h, scalar=logit[:, 6 + e:7 + e], in1=h,
                                         op0=ALU.mult, op1=ALU.mult).then_inc(hid_ready, 1)
                hidden_turned(nd + n)
            dve.wait_ge(down_done, 2)
            dve.tensor_tensor(hid[:, 0, :], x1[:, :], kv_ps[0][:, :], ALU.add).then_inc(out_ready, 1)


def kernel(**inputs):
    import numpy as np
    import concourse.bacc as bacc
    from concourse.bass_utils import run_bass_kernel_spmd

    a = {k: np.asarray(v) for k, v in inputs.items()}

    def by_in(w):
        n_out, n_in = w.shape
        return w.T.reshape(n_in // P, P, n_out).transpose(1, 0, 2)

    def blocks(w):
        b = np.zeros((P, GF), w.dtype)
        for h in range(GRP):
            b[HD * h:HD * (h + 1), FD * h:FD * (h + 1)] = w.T
        return b

    wo, wqkv, wswi = (by_in(a[n]).reshape(P, -1) for n in ("L0_xattn_Wo", "L0_attn_w_qkv", "L0_attn_w_swiglu"))
    early = np.concatenate([wo, wqkv, wswi], axis=1)
    pick = np.zeros((P, NPAIR, NH), np.float32)
    for j in range(NPAIR):
        pick[0:FD, j, 2 * j] = 1.0
        pick[FD:P, j, 2 * j + 1] = 1.0
    arrays = {
        "x": a["x"][0],
        "ctx": a["ctx_2048"][0].reshape(NC, CHUNK, KC, P).transpose(0, 3, 2, 1),
        "mask": a["mask_BxS2_ff1"][0].reshape(NT, P).T,
        "wq": by_in(a["L0_xattn_Wq"]),
        "bq": a["L0_xattn_bq"].reshape(KC, P).T,
        "wk": by_in(a["L0_xattn_Wk"]),
        "bk": a["L0_xattn_bk"].reshape(KC, P).T,
        "wv": by_in(a["L0_xattn_Wv"]),
        "bv": np.broadcast_to(a["L0_xattn_bv"], (P, D)),
        "bdq": blocks(a["L0_xattn_Wqf"]),
        "bdk": blocks(a["L0_xattn_Wkf"]),
        "bo": np.broadcast_to(a["L0_xattn_bo"], (P, D)),
        "early": early.reshape(P, NPIECE, PIECE).transpose(1, 0, 2),
        "wout": by_in(a["L0_attn_w_out"]),
        "wr": by_in(a["L0_ffn_w_router"]),
        "fc": np.stack([by_in(w) for w in a["L0_ffn_w_fc"]]),
        "proj": np.stack([by_in(w) for w in a["L0_ffn_w_proj"]]),
        "ident": np.eye(P, dtype=np.float32),
        "tri": np.triu(np.ones((P, P), np.float32)),
        "sel": pick,
    }
    arrays = {f"in_{k}": np.ascontiguousarray(v) for k, v in arrays.items()}
    nc = bacc.Bacc("TRN2", target_bir_lowering=False, num_devices=1)
    args = [nc.dram_tensor(k, v.shape, mybir.dt.from_np(v.dtype), kind="ExternalInput").ap()
            for k, v in arrays.items()]
    args.append(nc.dram_tensor("out_0", (1, P, D), mybir.dt.float32, kind="ExternalOutput").ap())
    perceiver_kernel(nc, *args)
    r = run_bass_kernel_spmd(nc, [arrays], core_ids=[0])
    return r.results[0]["out_0"]
```

```python
import concourse.bass as bass
from concourse import mybir
from contextlib import ExitStack

P = 128
D = 512
KC = D // P
NH = 16
HD = D // NH
FD = 64
NF = NH * FD
S_CTX = 12544
CHUNK = 256
TILES = CHUNK // P
NC = S_CTX // CHUNK
NT = S_CTX // P
GRP = P // HD
NG = NH // GRP
GF = GRP * FD
NPAIR = NF // P
PAIR = 2 * HD
JOBS = 4
DFF = 2048
LN_EPS = 1e-5
RMS_EPS = 1.1920929e-07
DEN_EPS = 1e-8
CUM_EPS = 1e-6

QKV_AT, SWI_AT = 0, KC * 3 * D
EARLY = SWI_AT + KC * 2 * DFF
PIECE = 1024
NPIECE = EARLY // PIECE
STAGE = EARLY - 8 * PIECE


def perceiver_kernel(nc, x_in, ctx_in, mask_in, wq_in, bq_in, wk_in, bk_in, wv_in, bv_in, bdq_in, bdk_in,
                     bo_in, wo_in, early_in, wout_in, wr_in, fc_in, proj_in, ident_in, tri_in, out):
    f32, f32r = mybir.dt.float32, mybir.dt.float32r
    ALU, ACT, AX = mybir.AluOpType, mybir.ActivationFunctionType, mybir.AxisListType

    ctx = ExitStack()
    with ctx:
        def sb(name, shape, dt=f32, where=ctx):
            return where.enter_context(nc.sbuf_tensor(name, shape, dt))

        def sem(name):
            return ctx.enter_context(nc.semaphore(name))

        early = sb("early", [P, EARLY])
        x_sb = sb("x_sb", [P, D])
        ident = sb("ident", [P, P])
        mask = sb("mask", [P, NT])
        bias_cols = sb("bias_cols", [P, 2 * KC])
        qf_T = sb("qf_T", [P, NPAIR, P])
        ksum_acc = sb("ksum_acc", [P, NF])
        stat = sb("stat", [P, 32])
        half = sb("half", [P, 1])
        ones = sb("ones", [P, 1])
        den = sb("den", [P, NH])
        rden = sb("rden", [P, NH])
        logit = sb("logit", [P, 8])
        w_router = sb("w_router", [P, KC, 2])

        phase = ExitStack()
        ctx_raw = sb("ctx_raw", [P, KC, CHUNK], f32, phase)
        ctx_hi = sb("ctx_hi", [P, 2, KC, CHUNK], f32r, phase)
        ctx_lo = sb("ctx_lo", [P, 2, KC, CHUNK], f32r, phase)
        wk_hi = sb("wk_hi", [P, KC, D], f32r, phase)
        wk_lo = sb("wk_lo", [P, KC, D], f32r, phase)
        wv_hi = sb("wv_hi", [P, KC, D], f32r, phase)
        wv_lo = sb("wv_lo", [P, KC, D], f32r, phase)
        bd = sb("bd", [P, 2, P], f32r, phase)
        keys_2 = sb("keys_2", [P, 2, NPAIR, CHUNK], f32r, phase)
        fb = sb("fb", [P, 2, 2, P], f32, phase)
        kf = sb("kf", [P, TILES, NPAIR, P], f32, phase)
        kf_2 = sb("kf_2", [P, TILES, NPAIR, 2, P], f32r, phase)
        v_2 = sb("v_2", [P, TILES, NPAIR, 2, PAIR], f32r, phase)
        phase.close()

        w_out = sb("w_out", [P, DFF // P, D])
        fc0 = sb("fc0", [P, KC, DFF])
        w_o = sb("w_o", [P, KC, D])
        bv = sb("bv", [P, D])
        bo = sb("bo", [P, D])
        tri = sb("tri", [P, P])
        kv_blocks = sb("kv_blocks", [P, NPAIR, P])
        kv_k = sb("kv_k", [P, NPAIR, P + 2])
        fold = sb("fold", [P, NPAIR, PAIR])
        att = sb("att", [P, D])
        act_T = sb("act_T", [P, KC, P])
        x1 = sb("x1", [P, D])
        z1 = sb("z1", [P, D])
        eq = sb("eq", [P, D])
        gate = sb("gate", [P, 2, D])
        hid = sb("hid", [P, 2, D])
        hid_T = sb("hid_T", [P, KC, P])
        wexp = kv_blocks[:, 0:4, :].rearrange("p a b -> p (a b)")
        wval = kv_blocks[:, 4:8, :].rearrange("p a b -> p (a b)")
        hid_T2 = [hid_T, kv_blocks[:, 0:4, :]]

        w_qkv = early[:, QKV_AT:SWI_AT].rearrange("p (k n) -> p k n", k=KC)
        w_swi = early[:, SWI_AT:EARLY].rearrange("p (k n) -> p k n", k=KC)
        late = early[:, SWI_AT:EARLY]
        proj0 = late[:, 0:KC * DFF].rearrange("p (k n) -> p k n", n=D)
        fc1 = late[:, KC * DFF:2 * KC * DFF].rearrange("p (k n) -> p k n", k=KC)

        def staged(at, n):
            return early[:, STAGE + at:STAGE + at + n]
        wq = staged(0, KC * D).rearrange("p (k n) -> p k n", k=KC)
        wk_raw = staged(KC * D, KC * D).rearrange("p (k n) -> p k n", k=KC)
        wv_raw = staged(2 * KC * D, KC * D).rearrange("p (k n) -> p k n", k=KC)
        z0 = staged(3 * KC * D, D)
        z0_T = staged(3 * KC * D + D, D).rearrange("p (k t) -> p k t", k=KC)
        q_T = staged(3 * KC * D + 2 * D, D).rearrange("p (k t) -> p k t", k=KC)
        bdq = staged(3 * KC * D + 3 * D, GF)
        bdk = staged(3 * KC * D + 3 * D + GF, P)

        def bank(name):
            return ctx.enter_context(nc.psum_tensor(name, [P, 512], f32))
        k_bank = bank("k_bank")
        v_bank = bank("v_bank")
        f_ps = [bank("f_ps0"), bank("f_ps1")]
        kv_ps = ctx.enter_context(nc.psum_tensor("kv_ps", [P, NPAIR, 2, P], f32))
        kv_bank = [kv_ps[:, 2 * b:2 * b + 2, :, :].rearrange("p a b c -> p (a b c)") for b in range(4)]
        k_ps, v_ps, down_ps = [k_bank[:, :], v_bank[:, :]], [kv_bank[1], kv_bank[2]], kv_bank[0]
        turn_ps = kv_bank[3]

        x_loaded = sem("x_loaded")
        ident_loaded = sem("ident_loaded")
        wk_loaded = sem("wk_loaded")
        bdk_loaded = sem("bdk_loaded")
        bias_loaded = sem("bias_loaded")
        wq_loaded = sem("wq_loaded")
        wv_loaded = sem("wv_loaded")
        mask_loaded = sem("mask_loaded")
        ctx_loaded = sem("ctx_loaded")
        early_loaded = sem("early_loaded")
        tail_small_loaded = sem("tail_small_loaded")
        wout_loaded = sem("wout_loaded")
        wo_loaded = sem("wo_loaded")
        fc0_loaded = sem("fc0_loaded")
        proj0_loaded = sem("proj0_loaded")
        fc1_loaded = sem("fc1_loaded")
        proj1_loaded = sem("proj1_loaded")
        out_stored = sem("out_stored")
        consts_set = sem("consts_set")
        chain = sem("vector_chain")
        act_chain = sem("scalar_chain")
        var_ready = sem("var_ready")
        rstd_ready = sem("rstd_ready")
        wk_hi_ready = sem("wk_hi_ready")
        wk_lo_ready = sem("wk_lo_ready")
        bd_hi_ready = sem("bd_hi_ready")
        bd_lo_ready = sem("bd_lo_ready")
        wv_hi_ready = sem("wv_hi_ready")
        wv_lo_ready = sem("wv_lo_ready")
        z0_ready = sem("z0_ready")
        z0T_done = sem("z0T_done")
        z0T_ready = sem("z0T_ready")
        q_done = sem("q_done")
        q_ready = sem("q_ready")
        qf_done = sem("qf_done")
        qf_ready = sem("qf_ready")
        ctx_hi_ready = sem("ctx_hi_ready")
        ctx_lo_ready = sem("ctx_lo_ready")
        k_done = sem("k_done")
        k_hi_ready = sem("k_hi_ready")
        k_lo_ready = sem("k_lo_ready")
        v_done = sem("v_done")
        v_hi_ready = sem("v_hi_ready")
        v_lo_ready = sem("v_lo_ready")
        f_done = sem("f_done")
        fb_ready = sem("fb_ready")
        fsum_ready = sem("fsum_ready")
        kf_ready = sem("kf_ready")
        kf_hi_ready = sem("kf_hi_ready")
        kf_lo_ready = sem("kf_lo_ready")
        ksum_added = sem("ksum_added")
        kv_done = sem("kv_done")
        ksumT_done = sem("ksumT_done")
        kvb_ready = sem("kvb_ready")
        kvT_done = sem("kvT_done")
        kvT_ready = sem("kvT_ready")
        kvb_zero = sem("kvb_zero")
        kvb_low = sem("kvb_low")
        ksum_ready = sem("ksum_ready")
        num_low = sem("num_low")
        num_done = sem("num_done")
        act_ready = sem("act_ready")
        actT_done = sem("actT_done")
        actT_ready = sem("actT_ready")
        o_done = sem("o_done")
        qkv_done = sem("qkv_done")
        rq_ready = sem("rq_ready")
        squares_ready = sem("squares_ready")
        expq_ready = sem("expq_ready")
        expk_ready = sem("expk_ready")
        wval_ready = sem("wval_ready")
        cum_done = sem("cum_done")
        g_done = sem("g_done")
        u_done = sem("u_done")
        expg_ready = sem("expg_ready")
        hid_ready = sem("hid_ready")
        hidT_done = sem("hidT_done")
        hidT_ready = sem("hidT_ready")
        down_done = sem("down_done")
        logit_done = sem("logit_done")
        logit_neg_ready = sem("logit_neg_ready")
        expl_ready = sem("expl_ready")
        fc_done = sem("fc_done")
        fc_half_ready = sem("fc_half_ready")
        out_ready = sem("out_ready")

        block = ctx.enter_context(nc.Block())


        @block.sync
        def _(sp):
            sp.dma_start(x_sb[:, :], x_in).then_inc(x_loaded, 16)
            sp.dma_start(wk_raw, wk_in).then_inc(wk_loaded, 16)
            sp.dma_start(ident[:, :], ident_in).then_inc(ident_loaded, 16)
            sp.dma_start(ctx_raw[:, :, :], ctx_in[0, :, :, :]).then_inc(ctx_loaded, 16)

            def load_chunk(c):
                sp.wait_ge(ctx_lo_ready, c)
                sp.dma_start(ctx_raw[:, :, :], ctx_in[c, :, :, :]).then_inc(ctx_loaded, 16)

            load_chunk(1)
            sp.wait_ge(wv_lo_ready, 1)
            sp.wait_ge(bd_lo_ready, 1)
            sp.wait_ge(qf_done, 2)
            with sp.Fori(2, 2 + NPIECE) as c:
                load_chunk(c)
                sp.dma_start(early[:, bass.ds((c - 2) * PIECE, PIECE)], early_in[c - 2, :, :])\
                  .then_inc(early_loaded, 16)
            with sp.Fori(2 + NPIECE, NC) as c:
                load_chunk(c)
            sp.wait_ge(kv_done, NT)
            sp.wait_ge(ksum_added, NT)
            sp.dma_start(w_o[:, :, :], wo_in).then_inc(wo_loaded, 16)
            sp.dma_start(bv[:, :], bv_in).then_inc(tail_small_loaded, 16)
            sp.dma_start(bo[:, :], bo_in).then_inc(tail_small_loaded, 16)
            sp.dma_start(tri[:, :], tri_in).then_inc(tail_small_loaded, 16)
            sp.dma_start(w_router[:, :, :], wr_in).then_inc(tail_small_loaded, 16)
            sp.dma_start(w_out[:, :, :], wout_in).then_inc(wout_loaded, 16)
            sp.dma_start(fc0[:, :, :], fc_in[0, :, :, :]).then_inc(fc0_loaded, 16)
            sp.wait_ge(u_done, 4)
            sp.dma_start(proj0, proj_in[0, :, :, :]).then_inc(proj0_loaded, 16)
            sp.dma_start(fc1, fc_in[1, :, :, :]).then_inc(fc1_loaded, 16)
            sp.wait_ge(down_done, 1)
            sp.dma_start(w_out[:, :, :], proj_in[1, :, :, :]).then_inc(proj1_loaded, 16)
            sp.wait_ge(out_ready, 1)
            sp.dma_start(out[0, :, :], hid[:, 0, :]).then_inc(out_stored, 16)
            sp.wait_ge(out_stored, 16)

        @block.gpsimd
        def _(pool):
            pool.memset(half[:, :], -0.5).then_inc(consts_set, 1)
            pool.memset(ones[:, :], 1.0).then_inc(consts_set, 1)
            pool.memset(ksum_acc[:, :], 0.0).then_inc(consts_set, 1)

            def rstd(n, col, m):
                pool.wait_ge(var_ready, n)
                pool.tensor_tensor(stat[:, col:col + m], stat[:, col:col + m],
                                   half[:, 0:1].to_broadcast([P, m]), ALU.pow).then_inc(rstd_ready, 1)

            def split_ctx_low(c, s):
                pool.wait_ge(ctx_hi_ready, c + 1)
                pool.tensor_tensor(ctx_lo[:, s, :, :], ctx_raw[:, :, :], ctx_hi[:, s, :, :].bitcast(f32),
                                   ALU.subtract).then_inc(ctx_lo_ready, 1)

            def add_features(n, t, first=False):
                pool.wait_ge(kf_ready, n + 1)
                pool.wait_ge(consts_set, 3) if first else pool.wait_ge(ksum_added, n)
                pool.tensor_tensor(ksum_acc[:, :].rearrange("p (j f) -> p j f", f=P),
                                   ksum_acc[:, :].rearrange("p (j f) -> p j f", f=P), kf[:, t, :, :], ALU.add)\
                    .then_inc(ksum_added, 1)

            def period(c, s, first=False, split=True):
                add_features(TILES * c, 0, first)
                if split:
                    split_ctx_low(c + 2, s)
                add_features(TILES * c + 1, 1)

            pool.wait_ge(consts_set, 3)
            rstd(1, 8, 1)
            split_ctx_low(0, 0)
            split_ctx_low(1, 1)
            period(0, 0, first=True)
            with pool.Fori(1, NC - 2, 2) as c:
                period(c, 1)
                period(c + 1, 0)
            period(NC - 2, 1, split=False)
            period(NC - 1, 0, split=False)
            pool.wait_ge(kv_done, NT)
            pool.wait_ge(ksum_added, NT)
            pool.memset(kv_blocks[:, :, :], 0.0).then_inc(kvb_zero, 1)
            pool.memset(kv_k[:, :, P:P + 2], 0.0).then_inc(kvb_zero, 1)
            rstd(2, 8, 1)
            rstd(3, 9, 1)
            rstd(4, 10, 2)
            rstd(5, 8, 1)

        @block.scalar
        def _(act):
            act.dma_start(bdk, bdk_in).then_inc(bdk_loaded, 16)
            act.dma_start(bias_cols[:, 0:KC], bq_in).then_inc(bias_loaded, 16)
            act.dma_start(bias_cols[:, KC:2 * KC], bk_in).then_inc(bias_loaded, 16)
            act.dma_start(wq, wq_in).then_inc(wq_loaded, 16)
            act.dma_start(bdq, bdq_in).then_inc(wq_loaded, 16)
            act.dma_start(wv_raw, wv_in).then_inc(wv_loaded, 16)
            act.dma_start(mask[:, :], mask_in).then_inc(mask_loaded, 16)

            def split_ctx_high(c, s):
                act.wait_ge(ctx_loaded, 16 * c + 16)
                act.activation(ctx_hi[:, s, :, :], ctx_raw[:, :, :], ACT.Copy).then_inc(ctx_hi_ready, 1)

            def keys_high(c, s, b):
                act.wait_ge(k_done, 2 * c + b + 1)
                for g in (2 * b, 2 * b + 1):
                    for h in range(2):
                        rows = slice(PAIR * h, PAIR * (h + 1))
                        last = act.activation(keys_2[rows, s, 2 * g + h, :],
                                              k_bank[rows, (g % 2) * CHUNK:(g % 2 + 1) * CHUNK],
                                              ACT.Identity, bias=bias_cols[rows, KC + g:KC + g + 1])
                last.then_inc(k_hi_ready, 1)

            def values_high(n, t, first):
                act.wait_ge(v_done, n + 1)
                if not first:
                    act.wait_ge(kv_done, n - 1)
                act.activation(v_2[:, t, :, 0, :], v_bank[:, :].rearrange("p (j e) -> p j e", e=PAIR),
                               ACT.Copy).then_inc(v_hi_ready, 1)

            def features_share(n, i, first):
                job = JOBS * n + i
                act.wait_ge(f_done, job + 1)
                if not (first and i < 2):
                    act.wait_ge(fsum_ready, job - 1)
                act.activation(fb[:, i % 2, :, :], f_ps[i % 2][:, :].rearrange("p (j x f) -> p j x f", j=2, x=2)
                               [:, :, 1, :], ACT.Copy).then_inc(fb_ready, 1)

            def features_high(n, t):
                act.wait_ge(kf_ready, n + 1)
                act.activation(kf_2[:, t, :, 0, :], kf[:, t, :, :], ACT.Copy).then_inc(kf_hi_ready, 1)

            def period(c, s, first=False, last=False, split=True):
                n = TILES * c
                features_share(n, 0, first)
                if not first:
                    features_high(n - 1, 1)
                features_share(n, 1, first)
                values_high(n, 0, first)
                for i in range(2, JOBS):
                    features_share(n, i, False)
                if not last:
                    keys_high(c + 1, 1 - s, 0)
                features_share(n + 1, 0, False)
                features_high(n, 0)
                features_share(n + 1, 1, False)
                values_high(n + 1, 1, first)
                if split:
                    split_ctx_high(c + 2, s)
                for i in range(2, JOBS):
                    features_share(n + 1, i, False)
                if not last:
                    keys_high(c + 1, 1 - s, 1)

            act.wait_ge(wk_loaded, 16)
            act.activation(wk_hi[:, :, :], wk_raw, ACT.Copy).then_inc(wk_hi_ready, 1)
            split_ctx_high(0, 0)
            act.wait_ge(bdk_loaded, 16)
            act.activation(bd[:, 0, :], bdk, ACT.Copy).then_inc(bd_hi_ready, 1)
            act.wait_ge(wv_loaded, 16)
            act.activation(wv_hi[:, :, :], wv_raw, ACT.Copy).then_inc(wv_hi_ready, 1)
            act.wait_ge(bias_loaded, 32)
            keys_high(0, 0, 0)
            split_ctx_high(1, 1)
            keys_high(0, 0, 1)
            period(0, 0, first=True)
            with act.Fori(1, NC - 2, 2) as c:
                period(c, 1)
                period(c + 1, 0)
            period(NC - 2, 1, split=False)
            period(NC - 1, 0, last=True, split=False)
            features_high(NT - 1, 1)

            act.wait_ge(kv_done, NT)
            act.wait_ge(ksum_added, NT)
            for b in range(2):
                for p in range(4):
                    rows, cols = slice(HD * p, HD * (p + 1)), slice(FD * (p % 2), FD * (p % 2 + 1))
                    last = act.activation(fold[rows, 4 * b:4 * b + 4, :], kv_ps[rows, 4 * b:4 * b + 4, 1, cols],
                                          ACT.Copy)
                last.then_inc(kvb_low, 1)
            act.wait_ge(kvT_done, 1)
            act.activation(kv_k[:, 0:4, 0:P], f_ps[0][:, :].rearrange("p (j e) -> p j e", e=P), ACT.Copy)\
               .then_inc(kvT_ready, 1)
            act.wait_ge(num_done, 1)
            for b in range(4):
                last = act.activation(fold[:, 2 * b:2 * b + 2, :],
                                      kv_bank[b][:, 0:2 * (P + 2)].rearrange("p (j e) -> p j e", j=2)
                                      [:, :, PAIR:2 * PAIR], ACT.Copy)
            last.then_inc(num_low, 1)
            act.wait_ge(qkv_done, 1)
            act.activation(eq[:, :], k_ps[0], ACT.Square, accum_out=stat[:, 10:11]).then_inc(act_chain, 1)
            act.wait_ge(act_chain, 1)
            act.wait_ge(qkv_done, 2)
            act.activation(eq[:, :], k_ps[1], ACT.Square, accum_out=stat[:, 11:12]).then_inc(squares_ready, 1)
            act.wait_ge(rq_ready, 1)
            act.wait_ge(squares_ready, 1)
            act.activation(eq[:, :], k_ps[0], ACT.Exp, scale=stat[:, 12:13]).then_inc(expq_ready, 1)
            act.activation(wexp, k_ps[1], ACT.Exp, scale=stat[:, 11:12]).then_inc(expk_ready, 1)
            for n in range(DFF // D):
                act.wait_ge(g_done, n + 1)
                if n >= 2:
                    act.wait_ge(hid_ready, n - 1)
                act.activation(gate[:, n % 2, :], k_ps[n % 2], ACT.Exp, scale=-1.0)\
                   .then_inc(expg_ready, 1)
            act.wait_ge(logit_neg_ready, 1)
            act.activation(logit[:, 3:5], logit[:, 0:2], ACT.Exp, bias=logit[:, 2:3]).then_inc(expl_ready, 1)
            for n in range(2 * DFF // D):
                act.wait_ge(fc_done, n + 1)
                if n >= 2:
                    act.wait_ge(hid_ready, DFF // D + n - 1)
                act.activation(gate[:, n % 2, :], k_ps[n % 2], ACT.Copy, scale=0.5)\
                   .then_inc(fc_half_ready, 1)

        @block.tensor
        def _(pe):
            def three(out_ps, st_hi, st_lo, mv_hi, mv_lo, start, stop, **kw):
                pe.matmul(out_ps, st_lo, mv_hi, start=start, stop=False, **kw)
                pe.matmul(out_ps, st_hi, mv_lo, start=False, stop=False, **kw)
                return pe.matmul(out_ps, st_hi, mv_hi, start=False, stop=stop, **kw)

            def keys(c, s, b, first=False, beside=None):
                pe.wait_ge(ctx_lo_ready, c + 1)
                if not first:
                    pe.wait_ge(k_lo_ready, 2 * c + b)
                for m in (2 * b, 2 * b + 1):
                    for k in range(KC):
                        last = three(k_bank[:, (m % 2) * CHUNK:(m % 2 + 1) * CHUNK],
                                     wk_hi[:, k, m * P:(m + 1) * P], wk_lo[:, k, m * P:(m + 1) * P],
                                     ctx_hi[:, s, k, :], ctx_lo[:, s, k, :], k == 0, k == KC - 1)
                        if m % 2 == 1 and k == KC - 1:
                            last.then_inc(k_done, 1)
                        if beside and k == 1:
                            feature_job(*beside, 2 + m % 2)

            def values(n, s, t, first, beside):
                if not first:
                    pe.wait_ge(v_lo_ready, n)
                for k in range(KC):
                    last = three(v_bank[:, :], ctx_hi[:, s, k, t * P:(t + 1) * P],
                                 ctx_lo[:, s, k, t * P:(t + 1) * P],
                                 wv_hi[:, k, :], wv_lo[:, k, :], k == 0, k == KC - 1)
                    if k == KC - 1:
                        last.then_inc(v_done, 1)
                    if k % 2 == 0:
                        feature_job(*beside, k // 2)

            def feature_job(c, s, t, first, i):
                if t == 0 and i % 2 == 0:
                    pe.wait_ge(k_lo_ready, 2 * c + i // 2 + 1)
                if not (first and t == 0 and i < 2):
                    pe.wait_ge(fsum_ready, JOBS * (TILES * c + t) + i - 1)
                for j in (2 * i, 2 * i + 1):
                    last = pe.matmul(f_ps[i % 2][:, (j % 2) * 2 * P:(j % 2 + 1) * 2 * P],
                                     keys_2[:, s, j, t * P:(t + 1) * P], bd[:, :, :].rearrange("p x f -> p (x f)"),
                                     start=True, stop=True)
                last.then_inc(f_done, 1)

            def key_values(n, t, first=False, last_tile=False):
                pe.wait_ge(v_lo_ready, n + 1)
                pe.wait_ge(kf_lo_ready, n + 1)
                for j in range(NPAIR):
                    last = pe.matmul(kv_ps[:, j, :, :].rearrange("p x f -> p (x f)"),
                                     v_2[:, t, j, :, :].rearrange("p x e -> p (x e)"),
                                     kf_2[:, t, j, :, :].rearrange("p x f -> p (x f)"),
                                     start=first and j % 2 == 0, stop=last_tile, skip_group_check=True)
                last.then_inc(kv_done, 1)

            def period(c, s, first=False, last=False):
                n = TILES * c
                for t in range(TILES):
                    beside = (c, s, t, first)
                    values(n + t, s, t, first and t == 0, beside)
                    if last:
                        feature_job(*beside, 2)
                        feature_job(*beside, 3)
                    else:
                        keys(c + 1, 1 - s, t, beside=beside)
                    if t == 1:
                        key_values(n, 0, first)
                    elif not first:
                        key_values(n - 1, 1)
                if last:
                    key_values(n + 1, 1, last_tile=True)

            def transposes(ps, src):
                for k in range(KC):
                    last = pe.transpose(ps[:, k * P:(k + 1) * P], src[:, k * P:(k + 1) * P], ident[:, :])
                return last

            def rows(ps, act_t, w, at, start=True, stop=True):
                for k in range(KC):
                    last = pe.matmul(ps, act_t[:, k, :], w[:, k, at:at + D], start=start and k == 0,
                                     stop=stop and k == KC - 1)
                return last

            pe.wait_ge(ident_loaded, 16)
            pe.wait_ge(z0_ready, 1)
            transposes(f_ps[0], z0).then_inc(z0T_done, 1)
            pe.wait_ge(wk_lo_ready, 1)
            keys(0, 0, 0, first=True)
            pe.wait_ge(z0T_ready, 1)
            pe.wait_ge(wq_loaded, 32)
            for m in range(KC):
                for k in range(KC):
                    last = pe.matmul(f_ps[1][:, m * P:(m + 1) * P], wq[:, k, m * P:(m + 1) * P],
                                     z0_T[:, k, :], start=k == 0, stop=k == KC - 1)
            last.then_inc(q_done, 1)
            keys(0, 0, 1)
            pe.wait_ge(q_ready, 1)
            for j in range(NPAIR):
                last = pe.matmul(kv_bank[j // 4][:, (j % 4) * P:(j % 4 + 1) * P], bdq[:, (j % 2) * P:(j % 2 + 1) * P],
                                 q_T[:, j // 2, :], start=True, stop=True)
                if j % 4 == 3:
                    last.then_inc(qf_done, 1)
            pe.wait_ge(qf_ready, 2)
            pe.wait_ge(bd_lo_ready, 1)
            pe.wait_ge(wv_lo_ready, 1)
            period(0, 0, first=True)
            with pe.Fori(1, NC - 2, 2) as c:
                period(c, 1)
                period(c + 1, 0)
            period(NC - 2, 1)
            period(NC - 1, 0, last=True)

            pe.wait_ge(ksum_added, NT)
            for j in range(NPAIR):
                last = pe.matmul(v_bank[:, j:j + 1], ksum_acc[:, j * P:(j + 1) * P], ones[:, :],
                                 start=True, stop=True)
            last.then_inc(ksumT_done, 1)
            for j in range(NPAIR):
                if j % 4 == 0:
                    pe.wait_ge(kvb_ready, j // 4 + 1)
                last = pe.transpose(f_ps[j // 4][:, (j % 4) * P:(j % 4 + 1) * P], kv_blocks[:, j, :], ident[:, :])
                if j % 4 == 3:
                    last.then_inc(kvT_done, 1)
            pe.wait_ge(ksum_ready, 1)
            pe.wait_ge(kvT_ready, 2)
            for j in range(NPAIR):
                last = pe.matmul(kv_bank[j // 2][:, (j % 2) * (P + 2):(j % 2 + 1) * (P + 2)], qf_T[:, j, :],
                                 kv_k[:, j, :], start=True, stop=True)
            last.then_inc(num_done, 1)

            def turn(n, src, ps):
                pe.wait_ge(act_ready, n)
                transposes(ps, src).then_inc(actT_done, 1)
                pe.wait_ge(actT_ready, n)

            turn(1, att, turn_ps)
            pe.wait_ge(wo_loaded, 16)
            rows(k_ps[1], act_T, w_o, 0).then_inc(o_done, 1)

            turn(2, att, turn_ps)
            pe.wait_ge(early_loaded, 16 * NPIECE)
            for n, ps in enumerate((k_ps[0], k_ps[1], v_ps[0])):
                rows(ps, act_T, w_qkv, n * D).then_inc(qkv_done, 1)
            pe.wait_ge(tail_small_loaded, 16 * 4)
            pe.wait_ge(expk_ready, 1)
            pe.matmul(f_ps[0][:, :], tri[:, :], wexp, start=True, stop=True).then_inc(cum_done, 1)
            pe.wait_ge(wval_ready, 1)
            pe.matmul(f_ps[1][:, :], tri[:, :], wval, start=True, stop=True).then_inc(cum_done, 1)
            turn(3, att, turn_ps)

            def hidden_turn(n):
                pe.wait_ge(hid_ready, n + 1)
                if n >= 2:
                    pe.wait_ge(hidT_ready, n - 1)
                transposes(f_ps[n % 2], hid[:, n % 2, :]).then_inc(hidT_done, 1)

            def hidden_down(n, w, at, first, last_one):
                pe.wait_ge(hidT_ready, n + 1)
                for k in range(KC):
                    last = pe.matmul(down_ps, hid_T2[n % 2][:, k, :], w[:, at + k, :],
                                     start=first and k == 0, stop=last_one and k == KC - 1)
                return last

            nd = DFF // D
            for n in range(nd + 1):
                if n < nd:
                    if n >= 2:
                        pe.wait_ge(hid_ready, n - 1)
                    rows(k_ps[n % 2], act_T, w_swi, DFF + n * D).then_inc(g_done, 1)
                    rows(v_ps[n % 2], act_T, w_swi, n * D).then_inc(u_done, 1)
                if n >= 1:
                    hidden_turn(n - 1)
                    if n == 1:
                        pe.wait_ge(wout_loaded, 16)
                    last = hidden_down(n - 1, w_out, (n - 1) * KC, n == 1, n == nd)
            last.then_inc(down_done, 1)

            turn(4, att, turn_ps)
            for k in range(KC):
                last = pe.matmul(v_ps[0][:, 0:2], act_T[:, k, :], w_router[:, k, :], start=k == 0,
                                 stop=k == KC - 1)
            last.then_inc(logit_done, 1)
            pe.wait_ge(fc0_loaded, 16)
            for n in range(2 * nd + 1):
                if n < 2 * nd:
                    if n == nd:
                        pe.wait_ge(fc1_loaded, 16)
                    if n >= 2:
                        pe.wait_ge(hid_ready, nd + n - 1)
                    rows(k_ps[n % 2], act_T, fc0 if n < nd else fc1, (n % nd) * D).then_inc(fc_done, 1)
                if n >= 1:
                    m = n - 1
                    hidden_turn(nd + m)
                    if m == 0:
                        pe.wait_ge(proj0_loaded, 16)
                    if m == nd:
                        pe.wait_ge(proj1_loaded, 16)
                    last = hidden_down(nd + m, proj0 if m < nd else w_out, (m % nd) * KC, m == 0, n == 2 * nd)
            last.then_inc(down_done, 1)

        @block.vector
        def _(dve):
            links = [0]

            def link(ins):
                links[0] += 1
                ins.then_inc(chain, 1)
                dve.wait_ge(chain, links[0])

            def layer_norm(n, dst, src):
                link(dve.bn_stats(stat[:, 0:6], src))
                link(dve.bn_aggr(stat[:, 6:8], stat[:, 0:6]))
                dve.tensor_scalar(stat[:, 8:9], stat[:, 7:8], LN_EPS, None, ALU.add).then_inc(var_ready, 1)
                dve.wait_ge(rstd_ready, n)
                return dve.tensor_scalar(dst, src, stat[:, 6:7], stat[:, 8:9], ALU.subtract, ALU.mult)

            def keys_low(c, s, b):
                dve.wait_ge(k_hi_ready, 2 * c + b + 1)
                for g in (2 * b, 2 * b + 1):
                    for h in range(2):
                        rows, other = slice(PAIR * h, PAIR * (h + 1)), slice(PAIR * (1 - h), PAIR * (2 - h))
                        last = dve.scalar_tensor_tensor(
                            out=keys_2[other, s, 2 * g + h, :],
                            in0=k_bank[rows, (g % 2) * CHUNK:(g % 2 + 1) * CHUNK],
                            scalar=bias_cols[rows, KC + g:KC + g + 1],
                            in1=keys_2[rows, s, 2 * g + h, :].bitcast(f32), op0=ALU.add, op1=ALU.subtract)
                last.then_inc(k_lo_ready, 1)

            def values_low(n, t):
                dve.wait_ge(v_hi_ready, n + 1)
                dve.tensor_tensor(v_2[:, t, :, 1, :], v_bank[:, :].rearrange("p (j e) -> p j e", e=PAIR),
                                  v_2[:, t, :, 0, :].bitcast(f32), ALU.subtract).then_inc(v_lo_ready, 1)

            def features_sum(n, t, i, first):
                if i == 0 and not first:
                    dve.wait_ge(ksum_added, n - 1)
                    dve.wait_ge(kf_lo_ready, n - 1)
                dve.wait_ge(fb_ready, JOBS * n + i + 1)
                dve.tensor_tensor(kf[:, t, 2 * i:2 * i + 2, :],
                                  f_ps[i % 2][:, :].rearrange("p (j x f) -> p j x f", j=2, x=2)[:, :, 0, :],
                                  fb[:, i % 2, :, :], ALU.add).then_inc(fsum_ready, 1)

            def masked_features(n, t):
                dve.wait_ge(fsum_ready, JOBS * n + JOBS)
                dve.tensor_scalar(kf[:, t, :, :], kf[:, t, :, :], 0.0, mask[:, bass.ds(n, 1)], ALU.max, ALU.mult)\
                   .then_inc(kf_ready, 1)

            def features_low(n, t):
                dve.wait_ge(kf_hi_ready, n + 1)
                dve.tensor_tensor(kf_2[:, t, :, 1, :], kf[:, t, :, :], kf_2[:, t, :, 0, :].bitcast(f32), ALU.subtract)\
                   .then_inc(kf_lo_ready, 1)

            def period(c, s, first=False, last=False):
                for t in range(TILES):
                    n = TILES * c + t
                    features_sum(n, t, 0, first)
                    if not (first and t == 0):
                        features_low(n - 1, 1 - t)
                    features_sum(n, t, 1, False)
                    values_low(n, t)
                    for i in range(2, JOBS):
                        features_sum(n, t, i, False)
                    masked_features(n, t)
                    if not last:
                        keys_low(c + 1, 1 - s, t)

            dve.wait_ge(x_loaded, 16)
            layer_norm(1, z0, x_sb[:, :]).then_inc(z0_ready, 1)
            dve.wait_ge(wk_hi_ready, 1)
            dve.tensor_tensor(wk_lo[:, :, :], wk_raw, wk_hi[:, :, :].bitcast(f32), ALU.subtract)\
               .then_inc(wk_lo_ready, 1)
            dve.wait_ge(z0T_done, 1)
            dve.tensor_copy(z0_T, f_ps[0][:, :].rearrange("p (k t) -> p k t", k=KC)).then_inc(z0T_ready, 1)
            dve.wait_ge(bd_hi_ready, 1)
            dve.tensor_tensor(bd[:, 1, :], bdk, bd[:, 0, :].bitcast(f32), ALU.subtract)\
               .then_inc(bd_lo_ready, 1)
            dve.wait_ge(wv_hi_ready, 1)
            dve.tensor_tensor(wv_lo[:, :, :], wv_raw, wv_hi[:, :, :].bitcast(f32), ALU.subtract)\
               .then_inc(wv_lo_ready, 1)
            dve.wait_ge(bias_loaded, 32)
            keys_low(0, 0, 0)
            dve.wait_ge(q_done, 1)
            for m in range(KC):
                last = dve.tensor_scalar(q_T[:, m, :], f_ps[1][:, m * P:(m + 1) * P], bias_cols[:, m:m + 1],
                                         None, ALU.add)
            last.then_inc(q_ready, 1)
            keys_low(0, 0, 1)
            for b in range(2):
                dve.wait_ge(qf_done, b + 1)
                dve.tensor_scalar(qf_T[:, 4 * b:4 * b + 4, :], kv_bank[b].rearrange("p (k t) -> p k t", k=4),
                                  0.0, None, ALU.max).then_inc(qf_ready, 1)
            dve.wait_ge(mask_loaded, 16)
            period(0, 0, first=True)
            with dve.Fori(1, NC - 2, 2) as c:
                period(c, 1)
                period(c + 1, 0)
            period(NC - 2, 1)
            period(NC - 1, 0, last=True)
            features_low(NT - 1, 1)

            dve.wait_ge(kvb_zero, 2)
            for b in range(2):
                dve.wait_ge(kvb_low, b + 1)
                for p in range(4):
                    rows, cols = slice(HD * p, HD * (p + 1)), slice(FD * (p % 2), FD * (p % 2 + 1))
                    last = dve.tensor_tensor(kv_blocks[rows, 4 * b:4 * b + 4, cols],
                                             kv_ps[rows, 4 * b:4 * b + 4, 0, cols],
                                             fold[rows, 4 * b:4 * b + 4, :], ALU.add)
                last.then_inc(kvb_ready, 1)
            dve.wait_ge(ksumT_done, 1)
            dve.tensor_copy(kv_k[0:FD, :, P], v_bank[0:FD, 0:NPAIR])
            dve.tensor_copy(kv_k[FD:P, :, P + 1], v_bank[FD:P, 0:NPAIR]).then_inc(ksum_ready, 1)
            dve.wait_ge(kvT_done, 2)
            dve.tensor_copy(kv_k[:, 4:8, 0:P], f_ps[1][:, :].rearrange("p (j e) -> p j e", e=P))\
               .then_inc(kvT_ready, 1)
            dve.wait_ge(num_low, 1)
            num = [kv_bank[b][:, 0:2 * (P + 2)].rearrange("p (j e) -> p j e", j=2) for b in range(4)]
            for b in range(4):
                last = dve.tensor_copy(den[:, 4 * b:4 * b + 4].rearrange("p (j h) -> p j h", j=2),
                                       num[b][:, :, P:P + 2])
            link(last)
            link(dve.tensor_scalar(rden[:, :], den[:, :], DEN_EPS, None, ALU.add))
            link(dve.reciprocal(rden[:, :], rden[:, :]))

            def by_head(a):
                return a.rearrange("p (h e) -> p h e", h=NH)

            def per_head(a):
                return a.unsqueeze(2).to_broadcast([P, NH, HD])
            dve.wait_ge(tail_small_loaded, 16 * 4)
            link(dve.tensor_tensor(by_head(att[:, :]), by_head(bv[:, :]), per_head(den[:, :]), ALU.mult))
            link(dve.tensor_tensor(att[:, :], att[:, :], fold[:, :, :].rearrange("p j e -> p (j e)"), ALU.add))
            for b in range(4):
                a = att[:, b * P:(b + 1) * P].rearrange("p (j e) -> p j e", j=2)
                last = dve.tensor_tensor(a, num[b][:, :, 0:PAIR], a, ALU.add)
            link(last)
            dve.tensor_tensor(by_head(att[:, :]), by_head(att[:, :]), per_head(rden[:, :]), ALU.mult)\
               .then_inc(act_ready, 1)

            def turned(n):
                dve.wait_ge(actT_done, n)
                dve.tensor_copy(act_T[:, :, :], turn_ps.rearrange("p (k t) -> p k t", k=KC))\
                   .then_inc(actT_ready, 1)
            turned(1)
            link(dve.tensor_tensor(x1[:, :], x_sb[:, :], bo[:, :], ALU.add))
            dve.wait_ge(o_done, 1)
            link(dve.tensor_tensor(x1[:, :], x1[:, :], k_ps[1], ALU.add))

            link(layer_norm(2, z1[:, :], x1[:, :]))
            link(dve.tensor_tensor(att[:, :], z1[:, :], z1[:, :], ALU.mult))
            link(dve.tensor_reduce(stat[:, 13:14], att[:, :], AX.X, ALU.add))
            dve.tensor_scalar(stat[:, 9:10], stat[:, 13:14], 1.0 / D, RMS_EPS, ALU.mult, ALU.add)\
               .then_inc(var_ready, 1)
            dve.wait_ge(rstd_ready, 3)
            dve.tensor_scalar(att[:, :], z1[:, :], stat[:, 9:10], None, ALU.mult).then_inc(act_ready, 1)
            turned(2)
            dve.wait_ge(squares_ready, 1)
            dve.tensor_scalar(stat[:, 10:12], stat[:, 10:12], 1.0 / D, RMS_EPS, ALU.mult, ALU.add)\
               .then_inc(var_ready, 1)
            dve.wait_ge(rstd_ready, 4)
            dve.tensor_scalar(stat[:, 12:13], stat[:, 10:11], -1.0, None, ALU.mult).then_inc(rq_ready, 1)
            dve.wait_ge(expk_ready, 1)
            dve.wait_ge(qkv_done, 3)
            dve.tensor_tensor(wval, v_ps[0], wexp, ALU.mult).then_inc(wval_ready, 1)
            dve.wait_ge(expq_ready, 1)
            link(dve.tensor_scalar(eq[:, :], eq[:, :], 1.0, None, ALU.add))
            dve.wait_ge(cum_done, 1)
            link(dve.scalar_tensor_tensor(out=eq[:, :], in0=f_ps[0][:, :], scalar=CUM_EPS, in1=eq[:, :],
                                          op0=ALU.add, op1=ALU.mult))
            link(dve.reciprocal(eq[:, :], eq[:, :]))
            dve.wait_ge(cum_done, 2)
            dve.tensor_tensor(att[:, :], f_ps[1][:, :], eq[:, :], ALU.mult).then_inc(act_ready, 1)
            turned(3)

            def hidden_turned(n):
                dve.wait_ge(hidT_done, n + 1)
                dve.tensor_copy(hid_T2[n % 2][:, :, :], f_ps[n % 2][:, :].rearrange("p (k t) -> p k t", k=KC))\
                   .then_inc(hidT_ready, 1)

            nd = DFF // D
            for n in range(nd):
                dve.wait_ge(expg_ready, n + 1)
                e = gate[:, n % 2, :]
                link(dve.tensor_scalar(e, e, 1.0, None, ALU.add))
                link(dve.reciprocal(e, e))
                link(dve.tensor_tensor(e, k_ps[n % 2], e, ALU.mult))
                dve.wait_ge(u_done, n + 1)
                dve.tensor_tensor(hid[:, n % 2, :], v_ps[n % 2], e, ALU.mult).then_inc(hid_ready, 1)
                if n == 0:
                    link(dve.tensor_tensor(x1[:, :], x1[:, :], z1[:, :], ALU.add))
                hidden_turned(n)
            dve.wait_ge(down_done, 1)
            link(dve.tensor_tensor(x1[:, :], x1[:, :], down_ps, ALU.add))

            layer_norm(5, att[:, :], x1[:, :]).then_inc(act_ready, 1)
            turned(4)
            dve.wait_ge(logit_done, 1)
            link(dve.tensor_copy(logit[:, 0:2], v_ps[0][:, 0:2]))
            link(dve.tensor_reduce(logit[:, 2:3], logit[:, 0:2], AX.X, ALU.max))
            dve.tensor_scalar(logit[:, 2:3], logit[:, 2:3], -1.0, None, ALU.mult).then_inc(logit_neg_ready, 1)
            dve.wait_ge(expl_ready, 1)
            link(dve.tensor_reduce(logit[:, 5:6], logit[:, 3:5], AX.X, ALU.add))
            link(dve.reciprocal(logit[:, 5:6], logit[:, 5:6]))
            link(dve.tensor_scalar(logit[:, 3:5], logit[:, 3:5], logit[:, 5:6], None, ALU.mult))
            link(dve.tensor_tensor(logit[:, 6:7], logit[:, 3:4], logit[:, 4:5], ALU.is_ge))
            link(dve.tensor_scalar(logit[:, 7:8], logit[:, 6:7], -1.0, 1.0, ALU.mult, ALU.add))
            link(dve.tensor_tensor(logit[:, 6:8], logit[:, 6:8], logit[:, 3:5], ALU.mult))

            for n in range(2 * nd):
                e = n // nd
                dve.wait_ge(fc_half_ready, n + 1)
                h = gate[:, n % 2, :]
                link(dve.tensor_tensor(h, k_ps[n % 2], h, ALU.max))
                dve.scalar_tensor_tensor(out=hid[:, n % 2, :], in0=h, scalar=logit[:, 6 + e:7 + e], in1=h,
                                         op0=ALU.mult, op1=ALU.mult).then_inc(hid_ready, 1)
                hidden_turned(nd + n)
            dve.wait_ge(down_done, 2)
            dve.tensor_tensor(hid[:, 0, :], x1[:, :], down_ps, ALU.add).then_inc(out_ready, 1)


def kernel(**inputs):
    import numpy as np
    import concourse.bacc as bacc
    from concourse.bass_utils import run_bass_kernel_spmd

    a = {k: np.asarray(v) for k, v in inputs.items()}

    def by_in(w):
        n_out, n_in = w.shape
        return w.T.reshape(n_in // P, P, n_out).transpose(1, 0, 2)

    def blocks(w, heads):
        b = np.zeros((HD * heads, FD * heads), w.dtype)
        for h in range(heads):
            b[HD * h:HD * (h + 1), FD * h:FD * (h + 1)] = w.T
        return b

    early = np.concatenate([by_in(a[n]).reshape(P, -1) for n in ("L0_attn_w_qkv", "L0_attn_w_swiglu")], axis=1)
    arrays = {
        "x": a["x"][0],
        "ctx": a["ctx_2048"][0].reshape(NC, CHUNK, KC, P).transpose(0, 3, 2, 1),
        "mask": a["mask_BxS2_ff1"][0].reshape(NT, P).T,
        "wq": by_in(a["L0_xattn_Wq"]),
        "bq": a["L0_xattn_bq"].reshape(KC, P).T,
        "wk": by_in(a["L0_xattn_Wk"]),
        "bk": a["L0_xattn_bk"].reshape(KC, P).T,
        "wv": by_in(a["L0_xattn_Wv"]),
        "bv": np.broadcast_to(a["L0_xattn_bv"], (P, D)),
        "bdq": blocks(a["L0_xattn_Wqf"], GRP),
        "bdk": np.tile(blocks(a["L0_xattn_Wkf"], 2), (2, 1)),
        "bo": np.broadcast_to(a["L0_xattn_bo"], (P, D)),
        "wo": by_in(a["L0_xattn_Wo"]),
        "early": early.reshape(P, NPIECE, PIECE).transpose(1, 0, 2),
        "wout": by_in(a["L0_attn_w_out"]),
        "wr": by_in(a["L0_ffn_w_router"]),
        "fc": np.stack([by_in(w) for w in a["L0_ffn_w_fc"]]),
        "proj": np.stack([by_in(w) for w in a["L0_ffn_w_proj"]]),
        "ident": np.eye(P, dtype=np.float32),
        "tri": np.triu(np.ones((P, P), np.float32)),
    }
    arrays = {f"in_{k}": np.ascontiguousarray(v) for k, v in arrays.items()}
    nc = bacc.Bacc("TRN2", target_bir_lowering=False, num_devices=1)
    args = [nc.dram_tensor(k, v.shape, mybir.dt.from_np(v.dtype), kind="ExternalInput").ap()
            for k, v in arrays.items()]
    args.append(nc.dram_tensor("out_0", (1, P, D), mybir.dt.float32, kind="ExternalOutput").ap())
    perceiver_kernel(nc, *args)
    r = run_bass_kernel_spmd(nc, [arrays], core_ids=[0])
    return r.results[0]["out_0"]
```

```python
import concourse.bass as bass
from concourse import mybir
from contextlib import ExitStack

P = 128
D = 512
KC = D // P
NH = 16
HD = D // NH
FD = 64
NF = NH * FD
S_CTX = 12544
CHUNK = 256
TILES = CHUNK // P
NC = S_CTX // CHUNK
NT = S_CTX // P
GRP = P // HD
NG = NH // GRP
GF = GRP * FD
NPAIR = NF // P
PAIR = 2 * HD
JOBS = 4
DFF = 2048
LN_EPS = 1e-5
RMS_EPS = 1.1920929e-07
DEN_EPS = 1e-8
CUM_EPS = 1e-6

QKV_AT, SWI_AT = 0, KC * 3 * D
EARLY = SWI_AT + KC * 2 * DFF
PIECE = 1024
NPIECE = EARLY // PIECE
STAGE = EARLY - 8 * PIECE


def perceiver_kernel(nc, x_in, ctx_in, mask_in, wq_in, bq_in, wk_in, bk_in, wv_in, bv_in, bdq_in, bdk_in,
                     bo_in, wo_in, early_in, wout_in, wr_in, fc_in, proj_in, ident_in, tri_in, fold_in, out):
    f32, f32r = mybir.dt.float32, mybir.dt.float32r
    ALU, ACT, AX = mybir.AluOpType, mybir.ActivationFunctionType, mybir.AxisListType

    ctx = ExitStack()
    with ctx:
        def sb(name, shape, dt=f32, where=ctx):
            return where.enter_context(nc.sbuf_tensor(name, shape, dt))

        def sem(name):
            return ctx.enter_context(nc.semaphore(name))

        early = sb("early", [P, EARLY])
        x_sb = sb("x_sb", [P, D])
        ident = sb("ident", [P, P])
        mask = sb("mask", [P, NT])
        bias_cols = sb("bias_cols", [P, 2 * KC])
        qf_T = sb("qf_T", [P, NPAIR, P])
        ksum_acc = sb("ksum_acc", [P, NF])
        stat = sb("stat", [P, 32])
        half = sb("half", [P, 1])
        ones = sb("ones", [P, 1])
        den = sb("den", [P, NH])
        rden = sb("rden", [P, NH])
        logit = sb("logit", [P, 8])
        w_router = sb("w_router", [P, KC, 2])

        phase = ExitStack()
        wk_hi = sb("wk_hi", [P, KC, D], f32r, phase)
        wk_lo = sb("wk_lo", [P, KC, D], f32r, phase)
        ctx_raw = sb("ctx_raw", [P, KC, CHUNK], f32, phase)
        ctx_hi = sb("ctx_hi", [P, 2, KC, CHUNK], f32r, phase)
        ctx_lo = sb("ctx_lo", [P, 2, KC, CHUNK], f32r, phase)
        wv_hi = sb("wv_hi", [P, KC, D], f32r, phase)
        wv_lo = sb("wv_lo", [P, KC, D], f32r, phase)
        bd = sb("bd", [P, 2, P], f32r, phase)
        keys_2 = sb("keys_2", [P, 2, NPAIR, CHUNK], f32r, phase)
        fb = sb("fb", [P, 2, 2, P], f32, phase)
        kf = sb("kf", [P, TILES, NPAIR, P], f32, phase)
        kf_2 = sb("kf_2", [P, TILES, NPAIR, 2, P], f32r, phase)
        v_2 = sb("v_2", [P, TILES, NPAIR, 2, PAIR], f32r, phase)
        phase.close()

        kv_parts = sb("kv_parts", [P, NPAIR, 2, P])
        kv_k = sb("kv_k", [P, NPAIR, PAIR])
        ksum_k = sb("ksum_k", [P, NPAIR, 2])
        fold_eye = sb("fold_eye", [P, PAIR])
        bv = sb("bv", [P, D])
        bo = sb("bo", [P, D])
        tri = sb("tri", [P, P])
        w_o = sb("w_o", [P, KC, D])
        w_out = sb("w_out", [P, DFF // P, D])
        fc0 = sb("fc0", [P, KC, DFF])
        att = sb("att", [P, D])
        act_T = sb("act_T", [P, KC, P])
        x1 = sb("x1", [P, D])
        z1 = sb("z1", [P, D])
        eq = sb("eq", [P, D])
        gate = sb("gate", [P, 2, D])
        hid = sb("hid", [P, 2, D])
        hid_T = sb("hid_T", [P, KC, P])
        wexp = kv_parts[:, 0:2, :, :].rearrange("p j x f -> p (j x f)")
        wval = kv_parts[:, 2:4, :, :].rearrange("p j x f -> p (j x f)")
        rcum = kv_parts[:, 4:6, :, :].rearrange("p j x f -> p (j x f)")
        hid_T2 = [hid_T, kv_parts[:, 0:2, :, :].rearrange("p j x f -> p (j x) f")]

        w_qkv = early[:, QKV_AT:SWI_AT].rearrange("p (k n) -> p k n", k=KC)
        w_swi = early[:, SWI_AT:EARLY].rearrange("p (k n) -> p k n", k=KC)
        late = early[:, SWI_AT:EARLY]
        proj0 = late[:, 0:KC * DFF].rearrange("p (k n) -> p k n", n=D)
        fc1 = late[:, KC * DFF:2 * KC * DFF].rearrange("p (k n) -> p k n", k=KC)

        def staged(at, n):
            return early[:, STAGE + at:STAGE + at + n]
        wq = staged(0, KC * D).rearrange("p (k n) -> p k n", k=KC)
        wk_raw = staged(KC * D, KC * D).rearrange("p (k n) -> p k n", k=KC)
        wv_raw = staged(2 * KC * D, KC * D).rearrange("p (k n) -> p k n", k=KC)
        z0 = staged(3 * KC * D, D)
        z0_T = staged(3 * KC * D + D, D).rearrange("p (k t) -> p k t", k=KC)
        q_T = staged(3 * KC * D + 2 * D, D).rearrange("p (k t) -> p k t", k=KC)
        bdq = staged(3 * KC * D + 3 * D, GF)
        bdk = staged(3 * KC * D + 3 * D + GF, P)

        def bank(name):
            return ctx.enter_context(nc.psum_tensor(name, [P, 512], f32))
        k_bank = bank("k_bank")
        v_bank = bank("v_bank")
        f_ps = [bank("f_ps0"), bank("f_ps1")]
        kv_ps = ctx.enter_context(nc.psum_tensor("kv_ps", [P, NPAIR, 2, P], f32))
        kv_bank = [kv_ps[:, 2 * b:2 * b + 2, :, :].rearrange("p a b c -> p (a b c)") for b in range(4)]
        k_ps, v_ps, down_ps = [k_bank[:, :], v_bank[:, :]], [kv_bank[1], kv_bank[2]], kv_bank[0]
        turn_ps = kv_bank[3]
        num_ps, den_ps = kv_bank[0], v_bank[:, NPAIR:NPAIR + NH]

        x_loaded = sem("x_loaded")
        ident_loaded = sem("ident_loaded")
        wk_loaded = [sem("wk_loaded0"), sem("wk_loaded1")]
        bdk_loaded = sem("bdk_loaded")
        bias_loaded = sem("bias_loaded")
        wq_loaded = sem("wq_loaded")
        wv_loaded = sem("wv_loaded")
        mask_loaded = sem("mask_loaded")
        ctx_loaded = sem("ctx_loaded")
        early_loaded = sem("early_loaded")
        tail_small_loaded = sem("tail_small_loaded")
        fold_loaded = sem("fold_loaded")
        wout_loaded = sem("wout_loaded")
        wo_loaded = sem("wo_loaded")
        fc0_loaded = sem("fc0_loaded")
        proj0_loaded = sem("proj0_loaded")
        fc1_loaded = sem("fc1_loaded")
        proj1_loaded = sem("proj1_loaded")
        out_stored = sem("out_stored")
        consts_set = sem("consts_set")
        chain = sem("vector_chain")
        var_ready = sem("var_ready")
        rstd_ready = sem("rstd_ready")
        wk_hi_ready = sem("wk_hi_ready")
        wk_lo_ready = sem("wk_lo_ready")
        bd_hi_ready = sem("bd_hi_ready")
        bd_lo_ready = sem("bd_lo_ready")
        wv_hi_ready = sem("wv_hi_ready")
        wv_lo_ready = sem("wv_lo_ready")
        z0_ready = sem("z0_ready")
        z0T_done = sem("z0T_done")
        z0T_ready = sem("z0T_ready")
        q_done = sem("q_done")
        q_ready = sem("q_ready")
        qf_done = sem("qf_done")
        qf_ready = sem("qf_ready")
        ctx_hi_ready = sem("ctx_hi_ready")
        ctx_lo_ready = sem("ctx_lo_ready")
        k_done = sem("k_done")
        k_hi_ready = sem("k_hi_ready")
        k_lo_ready = sem("k_lo_ready")
        v_done = sem("v_done")
        v_hi_ready = sem("v_hi_ready")
        v_lo_ready = sem("v_lo_ready")
        f_done = sem("f_done")
        fb_ready = sem("fb_ready")
        fsum_ready = sem("fsum_ready")
        kf_ready = sem("kf_ready")
        kf_hi_ready = sem("kf_hi_ready")
        kf_lo_ready = sem("kf_lo_ready")
        ksum_added = sem("ksum_added")
        kv_done = sem("kv_done")
        ksumT_done = sem("ksumT_done")
        kv_left = [sem("kv_left0"), sem("kv_left1")]
        kvT_done = sem("kvT_done")
        kvT_ready = sem("kvT_ready")
        kv_zero = sem("kv_zero")
        ksum_ready = sem("ksum_ready")
        den_done = sem("den_done")
        num_done = sem("num_done")
        act_ready = sem("act_ready")
        actT_done = sem("actT_done")
        actT_ready = sem("actT_ready")
        o_done = sem("o_done")
        qkv_done = sem("qkv_done")
        squares_ready = sem("squares_ready")
        gateq_ready = sem("gateq_ready")
        expk_ready = sem("expk_ready")
        wval_ready = sem("wval_ready")
        cum_done = sem("cum_done")
        g_done = sem("g_done")
        u_done = sem("u_done")
        gateg_ready = sem("gateg_ready")
        hid_ready = sem("hid_ready")
        hidT_done = sem("hidT_done")
        hidT_ready = sem("hidT_ready")
        down_done = sem("down_done")
        logit_done = sem("logit_done")
        logit_neg_ready = sem("logit_neg_ready")
        expl_ready = sem("expl_ready")
        fc_done = sem("fc_done")
        fc_half_ready = sem("fc_half_ready")
        out_ready = sem("out_ready")

        block = ctx.enter_context(nc.Block())


        @block.sync
        def _(sp):
            sp.dma_start(x_sb[:, :], x_in).then_inc(x_loaded, 16)
            for b in range(2):
                sp.dma_start(wk_raw[:, :, b * CHUNK:(b + 1) * CHUNK], wk_in[:, :, b * CHUNK:(b + 1) * CHUNK])\
                  .then_inc(wk_loaded[b], 16)
                if b == 0:
                    sp.dma_start(ctx_raw[:, :, :], ctx_in[0, :, :, :]).then_inc(ctx_loaded, 16)
            sp.dma_start(ident[:, :], ident_in).then_inc(ident_loaded, 16)

            def load_chunk(c):
                sp.wait_ge(ctx_lo_ready, c)
                sp.dma_start(ctx_raw[:, :, :], ctx_in[c, :, :, :]).then_inc(ctx_loaded, 16)

            load_chunk(1)
            sp.wait_ge(wv_lo_ready, 1)
            sp.wait_ge(bd_lo_ready, 1)
            sp.wait_ge(qf_done, 2)
            with sp.Fori(2, 2 + NPIECE) as c:
                load_chunk(c)
                sp.dma_start(early[:, bass.ds((c - 2) * PIECE, PIECE)], early_in[c - 2, :, :])\
                  .then_inc(early_loaded, 16)
            with sp.Fori(2 + NPIECE, NC) as c:
                load_chunk(c)
            sp.wait_ge(k_done, 2 * NC)
            sp.dma_start(fold_eye[:, :], fold_in).then_inc(fold_loaded, 16)
            sp.dma_start(bv[:, :], bv_in).then_inc(tail_small_loaded, 16)
            sp.dma_start(bo[:, :], bo_in).then_inc(tail_small_loaded, 16)
            sp.dma_start(tri[:, :], tri_in).then_inc(tail_small_loaded, 16)
            sp.dma_start(w_router[:, :, :], wr_in).then_inc(tail_small_loaded, 16)
            sp.wait_ge(kv_done, NT)
            sp.wait_ge(ksum_added, NT)
            sp.dma_start(w_o[:, :, :], wo_in).then_inc(wo_loaded, 16)
            sp.dma_start(w_out[:, :, :], wout_in).then_inc(wout_loaded, 16)
            sp.dma_start(fc0[:, :, :], fc_in[0, :, :, :]).then_inc(fc0_loaded, 16)
            sp.wait_ge(u_done, 4)
            sp.dma_start(proj0, proj_in[0, :, :, :]).then_inc(proj0_loaded, 16)
            sp.dma_start(fc1, fc_in[1, :, :, :]).then_inc(fc1_loaded, 16)
            sp.wait_ge(down_done, 1)
            sp.dma_start(w_out[:, :, :], proj_in[1, :, :, :]).then_inc(proj1_loaded, 16)
            sp.wait_ge(out_ready, 1)
            sp.dma_start(out[0, :, :], hid[:, 0, :]).then_inc(out_stored, 16)
            sp.wait_ge(out_stored, 16)

        @block.gpsimd
        def _(pool):
            pool.memset(half[:, :], -0.5).then_inc(consts_set, 1)
            pool.memset(ones[:, :], 1.0).then_inc(consts_set, 1)
            pool.memset(ksum_acc[:, :], 0.0).then_inc(consts_set, 1)

            def rstd(n, col, m):
                pool.wait_ge(var_ready, n)
                pool.tensor_tensor(stat[:, col:col + m], stat[:, col:col + m],
                                   half[:, 0:1].to_broadcast([P, m]), ALU.pow).then_inc(rstd_ready, 1)

            def split_ctx_low(c, s):
                pool.wait_ge(ctx_hi_ready, c + 1)
                pool.tensor_tensor(ctx_lo[:, s, :, :], ctx_raw[:, :, :], ctx_hi[:, s, :, :].bitcast(f32),
                                   ALU.subtract).then_inc(ctx_lo_ready, 1)

            def add_features(n, t, first=False):
                pool.wait_ge(kf_ready, n + 1)
                pool.wait_ge(consts_set, 3) if first else pool.wait_ge(ksum_added, n)
                pool.tensor_tensor(ksum_acc[:, :].rearrange("p (j f) -> p j f", f=P),
                                   ksum_acc[:, :].rearrange("p (j f) -> p j f", f=P), kf[:, t, :, :], ALU.add)\
                    .then_inc(ksum_added, 1)

            def period(c, s, first=False, split=True):
                add_features(TILES * c, 0, first)
                if split:
                    split_ctx_low(c + 2, s)
                add_features(TILES * c + 1, 1)

            pool.wait_ge(consts_set, 3)
            rstd(1, 8, 1)
            split_ctx_low(0, 0)
            split_ctx_low(1, 1)
            period(0, 0, first=True)
            with pool.Fori(1, NC - 2, 2) as c:
                period(c, 1)
                period(c + 1, 0)
            period(NC - 2, 1, split=False)
            pool.wait_ge(k_done, 2 * NC)
            pool.memset(kv_k[:, :, :], 0.0).then_inc(kv_zero, 1)
            pool.memset(ksum_k[:, :, :], 0.0).then_inc(kv_zero, 1)
            period(NC - 1, 0, split=False)
            rstd(2, 8, 2)
            rstd(3, 10, 1)
            rstd(4, 11, 1)
            rstd(5, 8, 1)

        @block.scalar
        def _(act):
            act.dma_start(bias_cols[:, 0:KC], bq_in).then_inc(bias_loaded, 16)
            act.dma_start(bias_cols[:, KC:2 * KC], bk_in).then_inc(bias_loaded, 16)
            act.dma_start(bdk, bdk_in).then_inc(bdk_loaded, 16)
            act.dma_start(wq, wq_in).then_inc(wq_loaded, 16)
            act.dma_start(bdq, bdq_in).then_inc(wq_loaded, 16)
            act.dma_start(wv_raw, wv_in).then_inc(wv_loaded, 16)
            act.dma_start(mask[:, :], mask_in).then_inc(mask_loaded, 16)

            def split_ctx_high(c, s):
                act.wait_ge(ctx_loaded, 16 * c + 16)
                act.activation(ctx_hi[:, s, :, :], ctx_raw[:, :, :], ACT.Copy).then_inc(ctx_hi_ready, 1)

            def keys_high(c, s, b):
                act.wait_ge(k_done, 2 * c + b + 1)
                for g in (2 * b, 2 * b + 1):
                    for h in range(2):
                        rows = slice(PAIR * h, PAIR * (h + 1))
                        last = act.activation(keys_2[rows, s, 2 * g + h, :],
                                              k_bank[rows, (g % 2) * CHUNK:(g % 2 + 1) * CHUNK],
                                              ACT.Identity, bias=bias_cols[rows, KC + g:KC + g + 1])
                last.then_inc(k_hi_ready, 1)

            def values_high(n, t, first):
                act.wait_ge(v_done, n + 1)
                if not first:
                    act.wait_ge(kv_done, n - 1)
                act.activation(v_2[:, t, :, 0, :], v_bank[:, :].rearrange("p (j e) -> p j e", e=PAIR),
                               ACT.Copy).then_inc(v_hi_ready, 1)

            def features_share(n, i, first):
                job = JOBS * n + i
                act.wait_ge(f_done, job + 1)
                if not (first and i < 2):
                    act.wait_ge(fsum_ready, job - 1)
                act.activation(fb[:, i % 2, :, :], f_ps[i % 2][:, :].rearrange("p (j x f) -> p j x f", j=2, x=2)
                               [:, :, 1, :], ACT.Copy).then_inc(fb_ready, 1)

            def features_high(n, t):
                act.wait_ge(kf_ready, n + 1)
                act.activation(kf_2[:, t, :, 0, :], kf[:, t, :, :], ACT.Copy).then_inc(kf_hi_ready, 1)

            def period(c, s, first=False, last=False, split=True):
                n = TILES * c
                features_share(n, 0, first)
                if not first:
                    features_high(n - 1, 1)
                features_share(n, 1, first)
                values_high(n, 0, first)
                for i in range(2, JOBS):
                    features_share(n, i, False)
                if not last:
                    keys_high(c + 1, 1 - s, 0)
                features_share(n + 1, 0, False)
                features_high(n, 0)
                features_share(n + 1, 1, False)
                if last:
                    features_share(n + 1, 2, False)
                    features_share(n + 1, 3, False)
                    features_high(n + 1, 1)
                values_high(n + 1, 1, first)
                if split:
                    split_ctx_high(c + 2, s)
                if not last:
                    features_share(n + 1, 2, False)
                    features_share(n + 1, 3, False)
                    keys_high(c + 1, 1 - s, 1)

            def split_wk_high(b):
                cols = slice(b * CHUNK, (b + 1) * CHUNK)
                act.wait_ge(wk_loaded[b], 16)
                act.activation(wk_hi[:, :, cols], wk_raw[:, :, cols], ACT.Copy).then_inc(wk_hi_ready, 1)

            split_wk_high(0)
            split_ctx_high(0, 0)
            split_wk_high(1)
            act.wait_ge(bdk_loaded, 16)
            act.activation(bd[:, 0, :], bdk, ACT.Copy).then_inc(bd_hi_ready, 1)
            act.wait_ge(wv_loaded, 16)
            act.activation(wv_hi[:, :, :], wv_raw, ACT.Copy).then_inc(wv_hi_ready, 1)
            act.wait_ge(bias_loaded, 32)
            keys_high(0, 0, 0)
            split_ctx_high(1, 1)
            keys_high(0, 0, 1)
            period(0, 0, first=True)
            with act.Fori(1, NC - 2, 2) as c:
                period(c, 1)
                period(c + 1, 0)
            period(NC - 2, 1, split=False)
            period(NC - 1, 0, last=True, split=False)

            act.wait_ge(kv_done, NT)
            for b in range(2):
                act.activation(kv_parts[:, 2 * b:2 * b + 2, :, :], kv_ps[:, 2 * b:2 * b + 2, :, :], ACT.Copy)\
                   .then_inc(kv_left[0], 1)
            act.wait_ge(kvT_done, 1)
            act.wait_ge(kv_zero, 2)
            for h in range(2):
                rows, cols = slice(FD * h, FD * (h + 1)), slice(HD * h, HD * (h + 1))
                last = act.activation(kv_k[rows, 0:4, cols],
                                      f_ps[0][rows, 0:4 * PAIR].rearrange("p (j e) -> p j e", e=PAIR)[:, :, cols],
                                      ACT.Copy)
            last.then_inc(kvT_ready, 1)
            act.wait_ge(qkv_done, 1)
            act.activation(eq[:, :], k_ps[1], ACT.Square, accum_out=stat[:, 10:11]).then_inc(squares_ready, 1)
            act.wait_ge(rstd_ready, 3)
            act.activation(wexp, k_ps[1], ACT.Exp, scale=stat[:, 10:11]).then_inc(expk_ready, 1)
            act.wait_ge(qkv_done, 2)
            act.wait_ge(squares_ready, 1)
            act.activation(eq[:, :], k_ps[0], ACT.Square, accum_out=stat[:, 11:12]).then_inc(squares_ready, 1)
            act.wait_ge(squares_ready, 2)
            act.wait_ge(rstd_ready, 4)
            act.activation(eq[:, :], k_ps[0], ACT.Sigmoid, scale=stat[:, 11:12]).then_inc(gateq_ready, 1)
            for n in range(DFF // D):
                act.wait_ge(g_done, n + 1)
                if n >= 2:
                    act.wait_ge(hid_ready, n - 1)
                act.activation(gate[:, n % 2, :], k_ps[n % 2], ACT.Sigmoid).then_inc(gateg_ready, 1)
            act.wait_ge(logit_neg_ready, 1)
            act.activation(logit[:, 3:5], logit[:, 0:2], ACT.Exp, bias=logit[:, 2:3]).then_inc(expl_ready, 1)
            for n in range(2 * DFF // D):
                act.wait_ge(fc_done, n + 1)
                if n >= 2:
                    act.wait_ge(hid_ready, DFF // D + n - 1)
                act.activation(gate[:, n % 2, :], k_ps[n % 2], ACT.Copy, scale=0.5)\
                   .then_inc(fc_half_ready, 1)

        @block.tensor
        def _(pe):
            def three(out_ps, st_hi, st_lo, mv_hi, mv_lo, start, stop, **kw):
                pe.matmul(out_ps, st_lo, mv_hi, start=start, stop=False, **kw)
                pe.matmul(out_ps, st_hi, mv_lo, start=False, stop=False, **kw)
                return pe.matmul(out_ps, st_hi, mv_hi, start=False, stop=stop, **kw)

            def keys(c, s, b, first=False, beside=None):
                pe.wait_ge(ctx_lo_ready, c + 1)
                if not first:
                    pe.wait_ge(k_lo_ready, 2 * c + b)
                for m in (2 * b, 2 * b + 1):
                    for k in range(KC):
                        last = three(k_bank[:, (m % 2) * CHUNK:(m % 2 + 1) * CHUNK],
                                     wk_hi[:, k, m * P:(m + 1) * P], wk_lo[:, k, m * P:(m + 1) * P],
                                     ctx_hi[:, s, k, :], ctx_lo[:, s, k, :], k == 0, k == KC - 1)
                        if m % 2 == 1 and k == KC - 1:
                            last.then_inc(k_done, 1)
                        if beside and k == 1:
                            feature_job(*beside, 2 + m % 2)

            def values(n, s, t, first, beside, all_jobs=False):
                if not first:
                    pe.wait_ge(v_lo_ready, n)
                for k in range(KC):
                    last = three(v_bank[:, :], ctx_hi[:, s, k, t * P:(t + 1) * P],
                                 ctx_lo[:, s, k, t * P:(t + 1) * P],
                                 wv_hi[:, k, :], wv_lo[:, k, :], k == 0, k == KC - 1)
                    if k == KC - 1:
                        last.then_inc(v_done, 1)
                    if all_jobs or k % 2 == 0:
                        feature_job(*beside, k if all_jobs else k // 2)

            def feature_job(c, s, t, first, i):
                if t == 0 and i % 2 == 0:
                    pe.wait_ge(k_lo_ready, 2 * c + i // 2 + 1)
                if not (first and t == 0 and i < 2):
                    pe.wait_ge(fsum_ready, JOBS * (TILES * c + t) + i - 1)
                for j in (2 * i, 2 * i + 1):
                    last = pe.matmul(f_ps[i % 2][:, (j % 2) * 2 * P:(j % 2 + 1) * 2 * P],
                                     keys_2[:, s, j, t * P:(t + 1) * P], bd[:, :, :].rearrange("p x f -> p (x f)"),
                                     start=True, stop=True)
                last.then_inc(f_done, 1)

            def key_values(n, t, first=False, last_tile=False):
                pe.wait_ge(v_lo_ready, n + 1)
                pe.wait_ge(kf_lo_ready, n + 1)
                for j in range(NPAIR):
                    last = pe.matmul(kv_ps[:, j, :, :].rearrange("p x f -> p (x f)"),
                                     v_2[:, t, j, :, :].rearrange("p x e -> p (x e)"),
                                     kf_2[:, t, j, :, :].rearrange("p x f -> p (x f)"),
                                     start=first and j % 2 == 0, stop=last_tile, skip_group_check=True)
                last.then_inc(kv_done, 1)

            def period(c, s, first=False, last=False):
                n = TILES * c
                for t in range(TILES):
                    beside = (c, s, t, first)
                    values(n + t, s, t, first and t == 0, beside, last and t == 1)
                    if last and t == 0:
                        feature_job(*beside, 2)
                        feature_job(*beside, 3)
                    elif not last:
                        keys(c + 1, 1 - s, t, beside=beside)
                    if t == 1:
                        if first:
                            pe.wait_ge(qf_ready, 2)
                        key_values(n, 0, first)
                    elif not first:
                        key_values(n - 1, 1)
                if last:
                    keep_warm(8)
                    key_values(n + 1, 1, last_tile=True)

            def keep_warm(n, by=None, of=None):
                for _ in range(n):
                    pe.matmul(k_bank[:, :], ident[:, :] if by is None else by, x_sb[:, :] if of is None else of,
                              start=True, stop=True)

            def transposes(ps, src):
                for k in range(KC):
                    last = pe.transpose(ps[:, k * P:(k + 1) * P], src[:, k * P:(k + 1) * P], ident[:, :])
                return last

            def rows(ps, act_t, w, at, start=True, stop=True):
                for k in range(KC):
                    last = pe.matmul(ps, act_t[:, k, :], w[:, k, at:at + D], start=start and k == 0,
                                     stop=stop and k == KC - 1)
                return last

            pe.wait_ge(consts_set, 3)
            keep_warm(6, ksum_acc[:, 0:P], ksum_acc[:, 0:D])
            pe.wait_ge(wk_lo_ready, 1)
            keys(0, 0, 0, first=True)
            pe.wait_ge(ident_loaded, 16)
            pe.wait_ge(z0_ready, 1)
            transposes(f_ps[0], z0).then_inc(z0T_done, 1)
            pe.wait_ge(z0T_ready, 1)
            pe.wait_ge(wq_loaded, 32)
            for m in range(KC):
                for k in range(KC):
                    last = pe.matmul(f_ps[1][:, m * P:(m + 1) * P], wq[:, k, m * P:(m + 1) * P],
                                     z0_T[:, k, :], start=k == 0, stop=k == KC - 1)
            last.then_inc(q_done, 1)
            pe.wait_ge(wk_lo_ready, 2)
            keys(0, 0, 1)
            pe.wait_ge(q_ready, 1)
            for j in range(NPAIR):
                last = pe.matmul(kv_bank[j // 4][:, (j % 4) * P:(j % 4 + 1) * P], bdq[:, (j % 2) * P:(j % 2 + 1) * P],
                                 q_T[:, j // 2, :], start=True, stop=True)
                if j % 4 == 3:
                    last.then_inc(qf_done, 1)
            pe.wait_ge(bd_lo_ready, 1)
            pe.wait_ge(wv_lo_ready, 1)
            period(0, 0, first=True)
            with pe.Fori(1, NC - 2, 2) as c:
                period(c, 1)
                period(c + 1, 0)
            period(NC - 2, 1)
            period(NC - 1, 0, last=True)

            pe.wait_ge(ksum_added, NT)
            for j in range(NPAIR):
                last = pe.matmul(v_bank[:, j:j + 1], ksum_acc[:, j * P:(j + 1) * P], ones[:, :],
                                 start=True, stop=True)
            last.then_inc(ksumT_done, 1)
            pe.wait_ge(fold_loaded, 16)
            for j in range(NPAIR):
                if j % 2 == 0:
                    pe.wait_ge(kv_left[j // 4], j % 4 // 2 + 1)
                for x in range(2):
                    last = pe.matmul(f_ps[j // 4][:, (j % 4) * PAIR:(j % 4 + 1) * PAIR], kv_parts[:, j, x, :],
                                     fold_eye[:, :], start=x == 0, stop=x == 1)
                if j % 4 == 3:
                    last.then_inc(kvT_done, 1)
            pe.wait_ge(ksum_ready, 1)
            for j in range(NPAIR):
                last = pe.matmul(den_ps[:, 2 * j:2 * j + 2], qf_T[:, j, :], ksum_k[:, j, :], start=True, stop=True)
            last.then_inc(den_done, 1)
            pe.wait_ge(kvT_ready, 2)
            for j in range(NPAIR):
                last = pe.matmul(num_ps[:, j * PAIR:(j + 1) * PAIR], qf_T[:, j, :], kv_k[:, j, :],
                                 start=True, stop=True)
            last.then_inc(num_done, 1)

            def turn(n, src, ps):
                pe.wait_ge(act_ready, n)
                transposes(ps, src).then_inc(actT_done, 1)
                pe.wait_ge(actT_ready, n)

            keep_warm(2)
            turn(1, att, turn_ps)
            pe.wait_ge(wo_loaded, 16)
            rows(k_ps[1], act_T, w_o, 0).then_inc(o_done, 1)
            keep_warm(7)

            turn(2, att, turn_ps)
            pe.wait_ge(early_loaded, 16 * NPIECE)
            rows(k_ps[1], act_T, w_qkv, D).then_inc(qkv_done, 1)
            rows(k_ps[0], act_T, w_qkv, 0).then_inc(qkv_done, 1)
            pe.wait_ge(tail_small_loaded, 16 * 4)
            pe.wait_ge(expk_ready, 1)
            pe.matmul(f_ps[0][:, :], tri[:, :], wexp, start=True, stop=True).then_inc(cum_done, 1)
            rows(v_ps[0], act_T, w_qkv, 2 * D).then_inc(qkv_done, 1)
            pe.wait_ge(wval_ready, 1)
            pe.matmul(f_ps[1][:, :], tri[:, :], wval, start=True, stop=True).then_inc(cum_done, 1)
            turn(3, att, turn_ps)

            def hidden_turn(n):
                pe.wait_ge(hid_ready, n + 1)
                if n >= 2:
                    pe.wait_ge(hidT_ready, n - 1)
                transposes(f_ps[n % 2], hid[:, n % 2, :]).then_inc(hidT_done, 1)

            def hidden_down(n, w, at, first, last_one):
                pe.wait_ge(hidT_ready, n + 1)
                for k in range(KC):
                    last = pe.matmul(down_ps, hid_T2[n % 2][:, k, :], w[:, at + k, :],
                                     start=first and k == 0, stop=last_one and k == KC - 1)
                return last

            nd = DFF // D
            for n in range(nd + 2):
                if n < nd:
                    if n >= 2:
                        pe.wait_ge(hid_ready, n - 1)
                    rows(k_ps[n % 2], act_T, w_swi, DFF + n * D).then_inc(g_done, 1)
                    rows(v_ps[n % 2], act_T, w_swi, n * D).then_inc(u_done, 1)
                if n >= 2:
                    if n == 2:
                        pe.wait_ge(wout_loaded, 16)
                    last = hidden_down(n - 2, w_out, (n - 2) * KC, n == 2, n == nd + 1)
                if 1 <= n <= nd:
                    hidden_turn(n - 1)
            last.then_inc(down_done, 1)

            keep_warm(6)
            turn(4, att, turn_ps)
            for k in range(KC):
                last = pe.matmul(v_ps[0][:, 0:2], act_T[:, k, :], w_router[:, k, :], start=k == 0,
                                 stop=k == KC - 1)
            last.then_inc(logit_done, 1)
            pe.wait_ge(fc0_loaded, 16)
            for n in range(2 * nd + 2):
                if n < 2 * nd:
                    if n == nd:
                        pe.wait_ge(fc1_loaded, 16)
                    if n >= 2:
                        pe.wait_ge(hid_ready, nd + n - 1)
                    rows(k_ps[n % 2], act_T, fc0 if n < nd else fc1, (n % nd) * D).then_inc(fc_done, 1)
                if n >= 2:
                    m = n - 2
                    if m == 0:
                        pe.wait_ge(proj0_loaded, 16)
                    if m == nd:
                        pe.wait_ge(proj1_loaded, 16)
                    last = hidden_down(nd + m, proj0 if m < nd else w_out, (m % nd) * KC, m == 0,
                                       n == 2 * nd + 1)
                if 1 <= n <= 2 * nd:
                    hidden_turn(nd + n - 1)
            last.then_inc(down_done, 1)

        @block.vector
        def _(dve):
            links = [0]

            def link(ins):
                links[0] += 1
                ins.then_inc(chain, 1)
                dve.wait_ge(chain, links[0])

            def layer_norm(n, dst, src):
                link(dve.bn_stats(stat[:, 0:6], src))
                link(dve.bn_aggr(stat[:, 6:8], stat[:, 0:6]))
                dve.tensor_scalar(stat[:, 8:9], stat[:, 7:8], LN_EPS, None, ALU.add).then_inc(var_ready, 1)
                dve.wait_ge(rstd_ready, n)
                return dve.tensor_scalar(dst, src, stat[:, 6:7], stat[:, 8:9], ALU.subtract, ALU.mult)

            def keys_low(c, s, b):
                dve.wait_ge(k_hi_ready, 2 * c + b + 1)
                for g in (2 * b, 2 * b + 1):
                    for h in range(2):
                        rows, other = slice(PAIR * h, PAIR * (h + 1)), slice(PAIR * (1 - h), PAIR * (2 - h))
                        last = dve.scalar_tensor_tensor(
                            out=keys_2[other, s, 2 * g + h, :],
                            in0=k_bank[rows, (g % 2) * CHUNK:(g % 2 + 1) * CHUNK],
                            scalar=bias_cols[rows, KC + g:KC + g + 1],
                            in1=keys_2[rows, s, 2 * g + h, :].bitcast(f32), op0=ALU.add, op1=ALU.subtract)
                last.then_inc(k_lo_ready, 1)

            def values_low(n, t):
                dve.wait_ge(v_hi_ready, n + 1)
                dve.tensor_tensor(v_2[:, t, :, 1, :], v_bank[:, :].rearrange("p (j e) -> p j e", e=PAIR),
                                  v_2[:, t, :, 0, :].bitcast(f32), ALU.subtract).then_inc(v_lo_ready, 1)

            def features_sum(n, t, i, first):
                if i == 0 and not first:
                    dve.wait_ge(ksum_added, n - 1)
                    dve.wait_ge(kf_lo_ready, n - 1)
                dve.wait_ge(fb_ready, JOBS * n + i + 1)
                dve.tensor_tensor(kf[:, t, 2 * i:2 * i + 2, :],
                                  f_ps[i % 2][:, :].rearrange("p (j x f) -> p j x f", j=2, x=2)[:, :, 0, :],
                                  fb[:, i % 2, :, :], ALU.add).then_inc(fsum_ready, 1)

            def masked_features(n, t):
                dve.wait_ge(fsum_ready, JOBS * n + JOBS)
                dve.tensor_scalar(kf[:, t, :, :], kf[:, t, :, :], 0.0, mask[:, bass.ds(n, 1)], ALU.max, ALU.mult)\
                   .then_inc(kf_ready, 1)

            def features_low(n, t):
                dve.wait_ge(kf_hi_ready, n + 1)
                dve.tensor_tensor(kf_2[:, t, :, 1, :], kf[:, t, :, :], kf_2[:, t, :, 0, :].bitcast(f32), ALU.subtract)\
                   .then_inc(kf_lo_ready, 1)

            def period(c, s, first=False, last=False):
                for t in range(TILES):
                    n = TILES * c + t
                    features_sum(n, t, 0, first)
                    if not (first and t == 0):
                        features_low(n - 1, 1 - t)
                    features_sum(n, t, 1, False)
                    early_jobs = last and t == 1
                    if not early_jobs:
                        values_low(n, t)
                    for i in range(2, JOBS):
                        features_sum(n, t, i, False)
                    masked_features(n, t)
                    if early_jobs:
                        features_low(n, t)
                        values_low(n, t)
                    if not last:
                        keys_low(c + 1, 1 - s, t)

            dve.wait_ge(x_loaded, 16)
            layer_norm(1, z0, x_sb[:, :]).then_inc(z0_ready, 1)
            for b in range(2):
                cols = slice(b * CHUNK, (b + 1) * CHUNK)
                dve.wait_ge(wk_hi_ready, b + 1)
                dve.tensor_tensor(wk_lo[:, :, cols], wk_raw[:, :, cols], wk_hi[:, :, cols].bitcast(f32),
                                  ALU.subtract).then_inc(wk_lo_ready, 1)
            dve.wait_ge(z0T_done, 1)
            dve.tensor_copy(z0_T, f_ps[0][:, :].rearrange("p (k t) -> p k t", k=KC)).then_inc(z0T_ready, 1)
            dve.wait_ge(bd_hi_ready, 1)
            dve.tensor_tensor(bd[:, 1, :], bdk, bd[:, 0, :].bitcast(f32), ALU.subtract)\
               .then_inc(bd_lo_ready, 1)
            dve.wait_ge(wv_hi_ready, 1)
            dve.tensor_tensor(wv_lo[:, :, :], wv_raw, wv_hi[:, :, :].bitcast(f32), ALU.subtract)\
               .then_inc(wv_lo_ready, 1)
            dve.wait_ge(bias_loaded, 32)
            keys_low(0, 0, 0)
            dve.wait_ge(q_done, 1)
            for m in range(KC):
                last = dve.tensor_scalar(q_T[:, m, :], f_ps[1][:, m * P:(m + 1) * P], bias_cols[:, m:m + 1],
                                         None, ALU.add)
            last.then_inc(q_ready, 1)
            keys_low(0, 0, 1)
            for b in range(2):
                dve.wait_ge(qf_done, b + 1)
                dve.tensor_scalar(qf_T[:, 4 * b:4 * b + 4, :], kv_bank[b].rearrange("p (k t) -> p k t", k=4),
                                  0.0, None, ALU.max).then_inc(qf_ready, 1)
            dve.wait_ge(mask_loaded, 16)
            period(0, 0, first=True)
            with dve.Fori(1, NC - 2, 2) as c:
                period(c, 1)
                period(c + 1, 0)
            period(NC - 2, 1)
            period(NC - 1, 0, last=True)

            dve.wait_ge(kv_done, NT)
            for b in (2, 3):
                dve.tensor_copy(kv_parts[:, 2 * b:2 * b + 2, :, :], kv_ps[:, 2 * b:2 * b + 2, :, :])\
                   .then_inc(kv_left[1], 1)
            dve.wait_ge(kv_zero, 2)
            dve.wait_ge(ksumT_done, 1)
            dve.tensor_copy(ksum_k[0:FD, :, 0], v_bank[0:FD, 0:NPAIR])
            dve.tensor_copy(ksum_k[FD:P, :, 1], v_bank[FD:P, 0:NPAIR]).then_inc(ksum_ready, 1)
            dve.wait_ge(kvT_done, 2)
            for h in range(2):
                rows, cols = slice(FD * h, FD * (h + 1)), slice(HD * h, HD * (h + 1))
                last = dve.tensor_copy(kv_k[rows, 4:8, cols],
                                       f_ps[1][rows, 0:4 * PAIR].rearrange("p (j e) -> p j e", e=PAIR)[:, :, cols])
            last.then_inc(kvT_ready, 1)
            dve.wait_ge(den_done, 1)
            link(dve.tensor_copy(den[:, :], den_ps))
            link(dve.tensor_scalar(rden[:, :], den[:, :], DEN_EPS, None, ALU.add))
            link(dve.reciprocal(rden[:, :], rden[:, :]))

            def by_head(a):
                return a.rearrange("p (h e) -> p h e", h=NH)

            def per_head(a):
                return a.unsqueeze(2).to_broadcast([P, NH, HD])
            dve.wait_ge(tail_small_loaded, 16 * 4)
            link(dve.tensor_tensor(by_head(att[:, :]), by_head(bv[:, :]), per_head(den[:, :]), ALU.mult))
            dve.wait_ge(num_done, 1)
            link(dve.tensor_tensor(att[:, :], num_ps, att[:, :], ALU.add))
            dve.tensor_tensor(by_head(att[:, :]), by_head(att[:, :]), per_head(rden[:, :]), ALU.mult)\
               .then_inc(act_ready, 1)

            def turned(n):
                dve.wait_ge(actT_done, n)
                dve.tensor_copy(act_T[:, :, :], turn_ps.rearrange("p (k t) -> p k t", k=KC))\
                   .then_inc(actT_ready, 1)
            turned(1)
            link(dve.tensor_tensor(x1[:, :], x_sb[:, :], bo[:, :], ALU.add))
            dve.wait_ge(o_done, 1)
            link(dve.tensor_tensor(x1[:, :], x1[:, :], k_ps[1], ALU.add))

            link(dve.bn_stats(stat[:, 0:6], x1[:, :]))
            link(dve.bn_aggr(stat[:, 6:8], stat[:, 0:6]))
            dve.tensor_scalar(stat[:, 8:9], stat[:, 7:8], LN_EPS, None, ALU.add)
            dve.tensor_scalar(stat[:, 9:10], stat[:, 7:8], 1.0 + RMS_EPS, RMS_EPS * LN_EPS, ALU.mult, ALU.add)\
               .then_inc(var_ready, 1)
            dve.wait_ge(rstd_ready, 2)
            dve.tensor_scalar(att[:, :], x1[:, :], stat[:, 6:7], stat[:, 9:10], ALU.subtract, ALU.mult)\
               .then_inc(act_ready, 1)
            link(dve.tensor_scalar(z1[:, :], x1[:, :], stat[:, 6:7], stat[:, 8:9], ALU.subtract, ALU.mult))
            link(dve.tensor_tensor(x1[:, :], x1[:, :], z1[:, :], ALU.add))
            turned(2)
            for i in range(2):
                dve.wait_ge(squares_ready, i + 1)
                dve.tensor_scalar(stat[:, 10 + i:11 + i], stat[:, 10 + i:11 + i], 1.0 / D, RMS_EPS,
                                  ALU.mult, ALU.add).then_inc(var_ready, 1)
            dve.wait_ge(cum_done, 1)
            link(dve.tensor_scalar(rcum, f_ps[0][:, :], CUM_EPS, None, ALU.add))
            link(dve.reciprocal(rcum, rcum))
            dve.wait_ge(qkv_done, 3)
            dve.tensor_tensor(wval, v_ps[0], wexp, ALU.mult).then_inc(wval_ready, 1)
            dve.wait_ge(gateq_ready, 1)
            link(dve.tensor_tensor(rcum, rcum, eq[:, :], ALU.mult))
            dve.wait_ge(cum_done, 2)
            dve.tensor_tensor(att[:, :], f_ps[1][:, :], rcum, ALU.mult).then_inc(act_ready, 1)
            turned(3)

            def hidden_turned(n):
                dve.wait_ge(hidT_done, n + 1)
                dve.tensor_copy(hid_T2[n % 2][:, :, :], f_ps[n % 2][:, :].rearrange("p (k t) -> p k t", k=KC))\
                   .then_inc(hidT_ready, 1)

            nd = DFF // D
            for n in range(nd):
                dve.wait_ge(gateg_ready, n + 1)
                e = gate[:, n % 2, :]
                link(dve.tensor_tensor(e, k_ps[n % 2], e, ALU.mult))
                dve.wait_ge(u_done, n + 1)
                dve.tensor_tensor(hid[:, n % 2, :], v_ps[n % 2], e, ALU.mult).then_inc(hid_ready, 1)
                hidden_turned(n)
            dve.wait_ge(down_done, 1)
            link(dve.tensor_tensor(x1[:, :], x1[:, :], down_ps, ALU.add))

            layer_norm(5, att[:, :], x1[:, :]).then_inc(act_ready, 1)
            turned(4)
            dve.wait_ge(logit_done, 1)
            link(dve.tensor_copy(logit[:, 0:2], v_ps[0][:, 0:2]))
            link(dve.tensor_reduce(logit[:, 2:3], logit[:, 0:2], AX.X, ALU.max))
            dve.tensor_scalar(logit[:, 2:3], logit[:, 2:3], -1.0, None, ALU.mult).then_inc(logit_neg_ready, 1)
            dve.wait_ge(expl_ready, 1)
            link(dve.tensor_reduce(logit[:, 5:6], logit[:, 3:5], AX.X, ALU.add))
            link(dve.reciprocal(logit[:, 5:6], logit[:, 5:6]))
            link(dve.tensor_scalar(logit[:, 3:5], logit[:, 3:5], logit[:, 5:6], None, ALU.mult))
            link(dve.tensor_tensor(logit[:, 6:7], logit[:, 3:4], logit[:, 4:5], ALU.is_ge))
            link(dve.tensor_scalar(logit[:, 7:8], logit[:, 6:7], -1.0, 1.0, ALU.mult, ALU.add))
            link(dve.tensor_tensor(logit[:, 6:8], logit[:, 6:8], logit[:, 3:5], ALU.mult))

            for n in range(2 * nd):
                e = n // nd
                dve.wait_ge(fc_half_ready, n + 1)
                h = gate[:, n % 2, :]
                link(dve.tensor_tensor(h, k_ps[n % 2], h, ALU.max))
                dve.scalar_tensor_tensor(out=hid[:, n % 2, :], in0=h, scalar=logit[:, 6 + e:7 + e], in1=h,
                                         op0=ALU.mult, op1=ALU.mult).then_inc(hid_ready, 1)
                hidden_turned(nd + n)
            dve.wait_ge(down_done, 2)
            dve.tensor_tensor(hid[:, 0, :], x1[:, :], down_ps, ALU.add).then_inc(out_ready, 1)


def kernel(**inputs):
    import numpy as np
    import concourse.bacc as bacc
    from concourse.bass_utils import run_bass_kernel_spmd

    a = {k: np.asarray(v) for k, v in inputs.items()}

    def by_in(w):
        n_out, n_in = w.shape
        return w.T.reshape(n_in // P, P, n_out).transpose(1, 0, 2)

    def blocks(w, heads):
        b = np.zeros((HD * heads, FD * heads), w.dtype)
        for h in range(heads):
            b[HD * h:HD * (h + 1), FD * h:FD * (h + 1)] = w.T
        return b

    early = np.concatenate([by_in(a[n]).reshape(P, -1) for n in ("L0_attn_w_qkv", "L0_attn_w_swiglu")], axis=1)
    arrays = {
        "x": a["x"][0],
        "ctx": a["ctx_2048"][0].reshape(NC, CHUNK, KC, P).transpose(0, 3, 2, 1),
        "mask": a["mask_BxS2_ff1"][0].reshape(NT, P).T,
        "wq": by_in(a["L0_xattn_Wq"]),
        "bq": a["L0_xattn_bq"].reshape(KC, P).T,
        "wk": by_in(a["L0_xattn_Wk"]),
        "bk": a["L0_xattn_bk"].reshape(KC, P).T,
        "wv": by_in(a["L0_xattn_Wv"]),
        "bv": np.broadcast_to(a["L0_xattn_bv"], (P, D)),
        "bdq": blocks(a["L0_xattn_Wqf"], GRP),
        "bdk": np.tile(blocks(a["L0_xattn_Wkf"], 2), (2, 1)),
        "bo": np.broadcast_to(a["L0_xattn_bo"], (P, D)),
        "wo": by_in(a["L0_xattn_Wo"]),
        "early": early.reshape(P, NPIECE, PIECE).transpose(1, 0, 2),
        "wout": by_in(a["L0_attn_w_out"]),
        "wr": by_in(a["L0_ffn_w_router"]),
        "fc": np.stack([by_in(w) for w in a["L0_ffn_w_fc"]]),
        "proj": np.stack([by_in(w) for w in a["L0_ffn_w_proj"]]),
        "ident": np.eye(P, dtype=np.float32),
        "tri": np.triu(np.ones((P, P), np.float32)),
        "fold": np.tile(np.eye(PAIR, dtype=np.float32), (2, 1)),
    }
    arrays = {f"in_{k}": np.ascontiguousarray(v) for k, v in arrays.items()}
    nc = bacc.Bacc("TRN2", target_bir_lowering=False, num_devices=1)
    args = [nc.dram_tensor(k, v.shape, mybir.dt.from_np(v.dtype), kind="ExternalInput").ap()
            for k, v in arrays.items()]
    args.append(nc.dram_tensor("out_0", (1, P, D), mybir.dt.float32, kind="ExternalOutput").ap())
    perceiver_kernel(nc, *args)
    r = run_bass_kernel_spmd(nc, [arrays], core_ids=[0])
    return r.results[0]["out_0"]
```
